# Optimizing a Trainium2 kernel written in Bass

```python
import numpy as np
import jax
import jax.numpy as jnp

def _softmax(x, axis=-1):
    return jax.nn.softmax(x, axis=axis)

def _gelu(x):
    return jax.nn.gelu(x, approximate=True)

def _silu(x):
    return jax.nn.silu(x)

def _sigmoid(x):
    return jax.nn.sigmoid(x)

def _layernorm(x, axis=-1, eps=1e-05):
    m = jnp.mean(x, axis=axis, keepdims=True)
    v = jnp.var(x, axis=axis, keepdims=True)
    return (x - m) / jnp.sqrt(v + eps)

def _scatter_add(tgt, idx, src, axis=0):
    return tgt.at[idx].add(src)

def _segment_sum(src, seg, n):
    return jax.ops.segment_sum(src, seg, n)
kernel_name = 'mk_cond_seq_d2_seqx_r4_fc61a9'

def setup_inputs(seed: int=0):
    np.random.seed(seed)
    _w = jnp.asarray

    def _rec_inputs():
        import jax
        import jax.numpy as jnp
        _rk = jax.random.key(seed)
        x = -7.109e-05 + 0.9999 * jax.random.normal(jax.random.fold_in(_rk, 1), (16, 256, 256), jnp.float32)
        _lenS = 256 - jax.random.randint(jax.random.fold_in(_rk, 7), (16,), 0, max(1, 256 // 4) + 1, jnp.int32)
        _lenS2 = 256 - jax.random.randint(jax.random.fold_in(_rk, 8), (16,), 0, max(1, 256 // 4) + 1, jnp.int32)
        condB_theta = jax.random.uniform(jax.random.fold_in(_rk, 11), (16,), jnp.float32, 0.0, 0.983423)
        condB_phi = jax.random.uniform(jax.random.fold_in(_rk, 12), (16,), jnp.float32, 0.0, 0.961312)
        itok_B_6_14 = jax.random.randint(jax.random.fold_in(_rk, 13), (16,), 6, 15, jnp.int32)
        return (x, condB_theta, condB_phi, itok_B_6_14)
    x, condB_theta, condB_phi, itok_B_6_14 = _rec_inputs()

    def _L0_cond_setup():
        import jax, jax.numpy as jnp
        import numpy as np
        key = jax.random.key(seed)
        k1, k2, k3 = jax.random.split(key, 3)
        B, N, D = (16, 1024, 256)
        embeddings = jax.random.normal(k1, (B, N, D), dtype=jnp.float32)
        theta = jax.random.uniform(k2, (B,), dtype=jnp.float32)
        phi = jax.random.uniform(k3, (B,), dtype=jnp.float32)
        return {'embeddings': embeddings, 'theta': theta, 'phi': phi}
    _L0_cond_all = _L0_cond_setup()
    _L0_cond_in = {k: v for k, v in _L0_cond_all.items() if k in ()}
    del _L0_cond_all

    def _L1_cond_setup():
        import jax, jax.numpy as jnp
        import numpy as np
        D = 256
        E = 8
        FF = 1024
        TOPK = 2
        S = 32
        SE = 64
        SH = 128
        B, T = (2, 512)

        def _forward(x, subject_ids, ln_g, ln_b, subj_emb, hyp_w1, hyp_b1, hyp_w2, hyp_b2, sty_w1, sty_b1, sty_w2, sty_b2, router_w, exp_w1, exp_b1, exp_w2, exp_b2):
            mu = x.mean(-1, keepdims=True)
            var = x.var(-1, keepdims=True)
            h = (x - mu) * jax.lax.rsqrt(var + 1e-05) * ln_g + ln_b
            m_t = h.mean(1, keepdims=True)
            v_t = h.var(1, keepdims=True)
            h_norm = (h - m_t) * jax.lax.rsqrt(v_t + 1e-08)
            se = subj_emb[subject_ids]
            hyp = jax.nn.relu(se @ hyp_w1 + hyp_b1) @ hyp_w2 + hyp_b2
            sty = jax.nn.relu(hyp @ sty_w1 + sty_b1) @ sty_w2 + sty_b2
            gamma, beta = jnp.split(sty, 2, axis=-1)
            gamma = jax.nn.softplus(gamma) + 1e-08
            h = h_norm * gamma[:, None, :] + beta[:, None, :]
            h_flat = h.reshape(-1, D)
            probs = jax.nn.softmax(h_flat @ router_w, axis=-1)
            gates, idx = jax.lax.top_k(probs, TOPK)
            gates = gates / gates.sum(-1, keepdims=True)
            N = h_flat.shape[0]
            combine = jnp.zeros((N, E), h_flat.dtype).at[jnp.arange(N)[:, None], idx].add(gates)
            hid = jax.nn.relu(jnp.einsum('nd,edf->nef', h_flat, exp_w1) + exp_b1)
            eout = jnp.einsum('nef,efd->ned', hid, exp_w2) + exp_b2
            y = jnp.einsum('ned,ne->nd', eout, combine)
            return x + y.reshape(x.shape)
        key = jax.random.key(seed)
        ks = jax.random.split(key, 16)
        n = lambda k, sh, s=0.02: jax.random.normal(k, sh, dtype=jnp.float32) * s
        return {'x': jax.random.normal(ks[0], (B, T, D), dtype=jnp.float32), 'subject_ids': jax.random.randint(ks[1], (B,), 0, S), 'ln_g': jnp.ones((D,), jnp.float32), 'ln_b': jnp.zeros((D,), jnp.float32), 'subj_emb': n(ks[2], (S, SE)), 'hyp_w1': n(ks[3], (SE, SH), 1.0 / np.sqrt(SE)), 'hyp_b1': jnp.zeros((SH,), jnp.float32), 'hyp_w2': n(ks[4], (SH, SH), 1.0 / np.sqrt(SH)), 'hyp_b2': jnp.zeros((SH,), jnp.float32), 'sty_w1': n(ks[5], (SH, SH // 2), 1.0 / np.sqrt(SH)), 'sty_b1': jnp.zeros((SH // 2,), jnp.float32), 'sty_w2': n(ks[6], (SH // 2, 2 * D), 1.0 / np.sqrt(SH // 2)), 'sty_b2': jnp.zeros((2 * D,), jnp.float32), 'router_w': n(ks[7], (D, E), 1.0 / np.sqrt(D)), 'exp_w1': n(ks[8], (E, D, FF), 1.0 / np.sqrt(D)), 'exp_b1': jnp.zeros((E, FF), jnp.float32), 'exp_w2': n(ks[9], (E, FF, D), 1.0 / np.sqrt(FF)), 'exp_b2': jnp.zeros((E, D), jnp.float32)}
    _L1_cond_all = _L1_cond_setup()
    _L1_cond_in = {k: v for k, v in _L1_cond_all.items() if k in ('ln_g', 'ln_b', 'subj_emb', 'hyp_w1', 'hyp_b1', 'hyp_w2', 'hyp_b2', 'sty_w1', 'sty_b1', 'sty_w2', 'sty_b2', 'router_w', 'exp_w1', 'exp_b1', 'exp_w2', 'exp_b2')}
    del _L1_cond_all
    return {'x': x, 'condB_theta': condB_theta, 'condB_phi': condB_phi, 'itok_B_6_14': itok_B_6_14, 'L1_cond_ln_g': _L1_cond_in['ln_g'], 'L1_cond_ln_b': _L1_cond_in['ln_b'], 'L1_cond_subj_emb': _L1_cond_in['subj_emb'], 'L1_cond_hyp_w1': _L1_cond_in['hyp_w1'], 'L1_cond_hyp_b1': _L1_cond_in['hyp_b1'], 'L1_cond_hyp_w2': _L1_cond_in['hyp_w2'], 'L1_cond_hyp_b2': _L1_cond_in['hyp_b2'], 'L1_cond_sty_w1': _L1_cond_in['sty_w1'], 'L1_cond_sty_b1': _L1_cond_in['sty_b1'], 'L1_cond_sty_w2': _L1_cond_in['sty_w2'], 'L1_cond_sty_b2': _L1_cond_in['sty_b2'], 'L1_cond_router_w': _L1_cond_in['router_w'], 'L1_cond_exp_w1': _L1_cond_in['exp_w1'], 'L1_cond_exp_b1': _L1_cond_in['exp_b1'], 'L1_cond_exp_w2': _L1_cond_in['exp_w2'], 'L1_cond_exp_b2': _L1_cond_in['exp_b2']}

def reference(x, condB_theta, condB_phi, itok_B_6_14, L1_cond_ln_g, L1_cond_ln_b, L1_cond_subj_emb, L1_cond_hyp_w1, L1_cond_hyp_b1, L1_cond_hyp_w2, L1_cond_hyp_b2, L1_cond_sty_w1, L1_cond_sty_b1, L1_cond_sty_w2, L1_cond_sty_b2, L1_cond_router_w, L1_cond_exp_w1, L1_cond_exp_b1, L1_cond_exp_w2, L1_cond_exp_b2):
    import jax
    import jax.numpy as jnp

    def _L0_cond_ref(embeddings, theta, phi):
        import jax, jax.numpy as jnp
        import numpy as np
        B, N, D = embeddings.shape
        e = embeddings.reshape(B, N, D // 4, 4)
        ct = jnp.cos(theta)[:, None, None]
        st = jnp.sin(theta)[:, None, None]
        cp = jnp.cos(phi)[:, None, None]
        sp = jnp.sin(phi)[:, None, None]
        x0, x1, x2, x3 = (e[..., 0], e[..., 1], e[..., 2], e[..., 3])
        out = jnp.stack([x0 * ct + x1 * st, -x0 * st + x1 * ct, x2 * cp + x3 * sp, -x2 * sp + x3 * cp], axis=-1)
        return out.reshape(B, N, D)

    def _L1_cond_ref(x, subject_ids, ln_g, ln_b, subj_emb, hyp_w1, hyp_b1, hyp_w2, hyp_b2, sty_w1, sty_b1, sty_w2, sty_b2, router_w, exp_w1, exp_b1, exp_w2, exp_b2):
        import jax, jax.numpy as jnp
        import numpy as np
        D = 256
        E = 8
        FF = 1024
        TOPK = 2
        S = 32
        SE = 64
        SH = 128
        B, T = (2, 512)

        def _forward(x, subject_ids, ln_g, ln_b, subj_emb, hyp_w1, hyp_b1, hyp_w2, hyp_b2, sty_w1, sty_b1, sty_w2, sty_b2, router_w, exp_w1, exp_b1, exp_w2, exp_b2):
            mu = x.mean(-1, keepdims=True)
            var = x.var(-1, keepdims=True)
            h = (x - mu) * jax.lax.rsqrt(var + 1e-05) * ln_g + ln_b
            m_t = h.mean(1, keepdims=True)
            v_t = h.var(1, keepdims=True)
            h_norm = (h - m_t) * jax.lax.rsqrt(v_t + 1e-08)
            se = subj_emb[subject_ids]
            hyp = jax.nn.relu(se @ hyp_w1 + hyp_b1) @ hyp_w2 + hyp_b2
            sty = jax.nn.relu(hyp @ sty_w1 + sty_b1) @ sty_w2 + sty_b2
            gamma, beta = jnp.split(sty, 2, axis=-1)
            gamma = jax.nn.softplus(gamma) + 1e-08
            h = h_norm * gamma[:, None, :] + beta[:, None, :]
            h_flat = h.reshape(-1, D)
            probs = jax.nn.softmax(h_flat @ router_w, axis=-1)
            gates, idx = jax.lax.top_k(probs, TOPK)
            gates = gates / gates.sum(-1, keepdims=True)
            N = h_flat.shape[0]
            combine = jnp.zeros((N, E), h_flat.dtype).at[jnp.arange(N)[:, None], idx].add(gates)
            hid = jax.nn.relu(jnp.einsum('nd,edf->nef', h_flat, exp_w1) + exp_b1)
            eout = jnp.einsum('nef,efd->ned', hid, exp_w2) + exp_b2
            y = jnp.einsum('ned,ne->nd', eout, combine)
            return x + y.reshape(x.shape)
        return _forward(x, subject_ids, ln_g, ln_b, subj_emb, hyp_w1, hyp_b1, hyp_w2, hyp_b2, sty_w1, sty_b1, sty_w2, sty_b2, router_w, exp_w1, exp_b1, exp_w2, exp_b2)
    x = _L0_cond_ref(x, condB_theta, condB_phi)
    x = _L1_cond_ref(x, itok_B_6_14, L1_cond_ln_g, L1_cond_ln_b, L1_cond_subj_emb, L1_cond_hyp_w1, L1_cond_hyp_b1, L1_cond_hyp_w2, L1_cond_hyp_b2, L1_cond_sty_w1, L1_cond_sty_b1, L1_cond_sty_w2, L1_cond_sty_b2, L1_cond_router_w, L1_cond_exp_w1, L1_cond_exp_b1, L1_cond_exp_w2, L1_cond_exp_b2)
    return x

_drawn_inputs = setup_inputs


def setup_inputs(seed=0):
    import zlib

    import numpy as np

    out = dict(_drawn_inputs(seed))
    spreads = {'L1_cond_ln_g': (1.0, 0.2),
     'L1_cond_ln_b': (0.0, 0.1),
     'L1_cond_hyp_b1': (0.0, 0.1),
     'L1_cond_hyp_b2': (0.0, 0.1),
     'L1_cond_sty_b1': (0.0, 0.1),
     'L1_cond_sty_b2': (0.0, 0.1),
     'L1_cond_exp_b1': (0.0, 0.1),
     'L1_cond_exp_b2': (0.0, 0.1)}
    factors = {}
    for name, (base, spread) in spreads.items():
        noise = np.random.default_rng([zlib.crc32(name.encode()), seed]).standard_normal(out[name].shape)
        drawn = base * np.exp(spread * noise) if base else spread * noise
        out[name] = jnp.asarray(drawn.astype(out[name].dtype))
    for name, factor in factors.items():
        out[name] = (out[name] * factor).astype(out[name].dtype)
    return out
```

```python
from contextlib import ExitStack

import concourse.bass as bass
from concourse import mybir

ALU = mybir.AluOpType
ACT = mybir.ActivationFunctionType
AX_X = mybir.AxisListType.X
F32 = mybir.dt.float32
F32R = mybir.dt.float32r
BF16 = mybir.dt.bfloat16
I32 = mybir.dt.int32
U32 = mybir.dt.uint32

P = 128
B, S, D = 16, 256, 256
N = B * S
E, FF, TOPK = 8, 1024, 2
SUBJ, SE, SH = 32, 64, 128
DC = D // P
FC = FF // P
PAIRS = B // 2
PT = 2 * S // P
GROUPS = PAIRS // 2
GT = 2 * PT
CAP = N + P
ROW = D + E + 1
MAXT = N * TOPK // P + E - 1
UNROLL = 4
STAGES = 4
PEEL = STAGES - 1 + UNROLL
WE = DC * FF + FC * D
BE = FF + D
NB = 512
LN_EPS, IN_EPS, SOFTPLUS_EPS = 1e-5, 1e-8, 1e-8
TWO_PI_A, TWO_PI_B = 6.28125, 0.0019353071795864769
HALF_PI = 1.5707963267948966
FAR = -3.0e38
T_EXPERT, T_NEED, T_SLOT, T_BASE, T_SPLIT, T_LOAD, T_OTHER = range(7)
assert (MAXT - PEEL) % UNROLL == 0


def moe_kernel(nc, x, theta, phi, itok, ln_g, ln_b, subj_emb, hyp_w1, hyp_b1, hyp_w2, hyp_b2,
               sty_w1, sty_b1, sty_w2, sty_b2, router_w, exp_w1, exp_b1, exp_w2, exp_b2, out):
    sent = nc.dram_tensor("sent_rows", (E * CAP + P, ROW), F32).ap()
    x_pairs = x.rearrange("(n j) (i p) d -> n p (j i) d", j=2, p=P)
    out_pairs = out[0:N, :].rearrange("(n i p) d -> n p i d", i=PT, p=P)

    with ExitStack() as ctx:
        def sb(name, shape, dt=F32):
            return ctx.enter_context(nc.sbuf_tensor(name, shape, dt))

        def sem(name):
            return ctx.enter_context(nc.semaphore(name))

        ident = sb("ident", [P, P])
        before = sb("before", [P, P], BF16)
        ones = sb("ones", [P, P], BF16)
        iota_p = sb("iota_p", [P, 1])
        rev = sb("rev", [P, E])
        ebase = sb("ebase", [P, E])
        tok = sb("tok", [P, GT])
        pad_row = sb("pad_row", [P, ROW])
        thresholds = sb("thresholds", [1, N // P])
        upto = sb("upto", [1, E, E])
        tiles = sb("tiles", [1, MAXT])
        th = sb("th", [P, 2, B])
        g_c = sb("g_c", [P, DC])
        b_c = sb("b_c", [P, DC])
        rw = sb("rw", [P, DC, E])
        ids_i = sb("ids_i", [SUBJ, B], I32)
        ids = sb("ids", [SUBJ, B])
        onehot = sb("onehot", [SUBJ, B])
        emb = sb("emb", [SUBJ, SE])
        hw1 = sb("hw1", [SE, SH])
        hw2 = sb("hw2", [SH, SH])
        sw1 = sb("sw1", [SH, SH // 2])
        sw2 = sb("sw2", [SH // 2, 2 * D])
        hb1 = sb("hb1", [SH, 1])
        hb2 = sb("hb2", [SH, 1])
        sb1 = sb("sb1", [SH // 2, 1])
        sb2 = sb("sb2", [P, 2 * DC])
        se_t = sb("se_t", [SE, B])
        hyp1 = sb("hyp1", [SH, B])
        hyp2 = sb("hyp2", [SH, B])
        sty1 = sb("sty1", [SH // 2, B])
        sty = sb("sty", [P, 2 * DC, B])
        soft = sb("soft", [P, 3, DC, B])
        gamma = sb("gamma", [P, B, DC])
        beta = sb("beta", [P, B, DC])
        turns_i = sb("turns_i", [P, 2, B], I32)
        turns = sb("turns", [P, 2, B])
        red = sb("red", [P, 2, B])
        co_arg = sb("co_arg", [P, 2, B])
        sn = sb("sn", [P, 2, B])
        cs = sb("cs", [P, 2, B])
        nsn = sb("nsn", [P, 2, B])
        xin = sb("xin", [P, 2, PT, D])
        xr = sb("xr", [P, 3, PT, D])
        z = sb("z", [P, 2, PT, D])
        h_t = sb("h_t", [P, 2, DC, PT * P])
        st = sb("st", [P, PT, 6])
        mv = sb("mv", [P, PT, 2])
        var_e = sb("var_e", [P, 2, 2 * DC])
        log_v = sb("log_v", [P, 2, 2 * DC])
        rs0 = sb("rs0", [P, 2, 2 * DC])
        sq = sb("sq", [P, 2 * DC])
        rstd = sb("rstd", [P, 2 * DC])
        rs_t = sb("rs_t", [P, 2 * DC])
        st_t = sb("st_t", [P, 2 * DC, 6])
        mv_t = sb("mv_t", [P, 2 * DC, 2])
        g4 = sb("g4", [P, 2, DC])
        b4 = sb("b4", [P, 2, DC])
        gg4 = sb("gg4", [P, 2, DC])
        tmp4 = sb("tmp4", [P, 6, 2 * DC])
        co_a = sb("co_a", [P, 2, 2 * DC])
        co_b = sb("co_b", [P, 2, 2 * DC])
        rows = sb("rows", [P, GT, ROW])
        lg = sb("lg", [P, GT, E])
        lg2 = sb("lg2", [P, GT, E])
        pick = sb("pick", [P, GT, E])
        oh1 = sb("oh1", [P, GT, E])
        oh2 = sb("oh2", [P, GT, E])
        mask = sb("mask", [P, GT, E], BF16)
        mx1 = sb("mx1", [P, GT])
        mx2 = sb("mx2", [P, GT])
        at1 = sb("at1", [P, GT])
        at2 = sb("at2", [P, GT])
        dm = sb("dm", [P, GT])
        ex = sb("ex", [P, GT])
        den = sb("den", [P, GT])
        gate1 = sb("gate1", [P, GT])
        gate2 = sb("gate2", [P, GT])
        comb1 = sb("comb1", [P, GT, E])
        comb2 = sb("comb2", [P, GT, E])
        place = sb("place", [P, GT, E])
        slot_f = sb("slot_f", [P, TOPK, GT])
        slot_u = sb("slot_u", [P, TOPK, GT], U32)
        carry = sb("carry", [P, E])
        pad_f = sb("pad_f", [P, E])
        pad_u = sb("pad_u", [P, E], U32)
        cnt = sb("cnt", [1, E])
        over = sb("over", [1, E, N // P])
        n_t = sb("n_t", [1, E])
        cum = sb("cum", [1, E, E])
        end = sb("end", [1, E])
        past = sb("past", [1, MAXT, E])
        pastn = sb("pastn", [1, MAXT, E])
        done_e = sb("done_e", [1, MAXT])
        start_t = sb("start_t", [1, MAXT])
        tf = sb("tf", [1, 9, MAXT])
        table = sb("table", [1, 7, MAXT + UNROLL], I32)
        stage = sb("stage", [P, WE + BE])
        wts = sb("wts", [P, 2 * 2 * WE], F32R)
        bias = sb("bias", [P, 2 * BE])
        got = sb("got", [P, UNROLL, ROW])
        gate = sb("gate", [P, UNROLL])
        dest = sb("dest", [P, UNROLL], U32)
        hin_hi = sb("hin_hi", [P, 2, D], F32R)
        hin_lo = sb("hin_lo", [P, 2, D], F32R)
        hid = sb("hid", [P, 2, FF])
        hid_hi = sb("hid_hi", [P, 2, FF], F32R)
        hid_lo = sb("hid_lo", [P, 2, FF], F32R)
        y_raw = sb("y_raw", [P, UNROLL, D])
        y = sb("y", [P, UNROLL, D])

        ps = ctx.enter_context(nc.psum_tensor("ps", [P, 8, NB], F32))
        zt_ps = [ps[:, 0:2, :], ps[:, 2:4, :]]
        back_ps = ps[:, 4:6, :]
        logit_ps = ps[:, 6, 0:GT * E]
        rank_ps = ps[:, 7, 0:(GT + 1) * E].rearrange("p (i e) -> p i e", e=E)
        style_ps = ps[:, 5, :]
        hin_ps = ps[:, 0, 0:D]
        hid_ps = ps[:, 1:3, :]
        hidt_ps = ps[:, 3:5, :]
        y_ps = [ps[:, 5, 0:D], ps[:, 6, 0:D]]

        small_in = sem("small_in")
        x_in = [sem("x_in0"), sem("x_in1")]
        consts = sem("consts")
        pad_ready = sem("pad_ready")
        angle = sem("angle")
        trig = sem("trig")
        style_mm = sem("style_mm")
        style_sb = sem("style_sb")
        soft_in = sem("soft_in")
        soft_ex = sem("soft_ex")
        soft_p1 = sem("soft_p1")
        soft_ln = sem("soft_ln")
        scaled = sem("scaled")
        rotated = sem("rotated")
        x_out = [sem("x_out0"), sem("x_out1"), sem("x_out2")]
        var_ready = [sem("var_ready_ln"), sem("var_ready_time")]
        log_ready = [sem("log_ready_ln"), sem("log_ready_time")]
        rs0_ready = [sem("rs0_ready_ln"), sem("rs0_ready_time")]
        normed = sem("normed")
        turned = sem("turned")
        coefs = sem("coefs")
        h_ready = sem("h_ready")
        turned_back = sem("turned_back")
        rows_filled = sem("rows_filled")
        logits_read = sem("logits_read")
        dm_ready = sem("dm_ready")
        ex_ready = sem("ex_ready")
        mask_ready = sem("mask_ready")
        ranks = sem("ranks")
        slots_ready = sem("slots_ready")
        rows_sent = [sem("rows_sent0"), sem("rows_sent1")]
        pad_idx = sem("pad_idx")
        pads_first = sem("pads_first")
        pads_rest = sem("pads_rest")
        pads_fixed = sem("pads_fixed")
        table_ready = sem("table_ready")
        stage_in = sem("stage_in")
        w_high = sem("w_high")
        w_ready = sem("w_ready")
        got_in = [sem(f"got_in{i}") for i in range(UNROLL)]
        hin_t = sem("hin_t")
        hin_high = sem("hin_high")
        hin_low = sem("hin_low")
        l1_done = sem("l1_done")
        hid_biased = sem("hid_biased")
        hidt_done = sem("hidt_done")
        hid_high = sem("hid_high")
        hid_low = sem("hid_low")
        l2_done = sem("l2_done")
        meta = sem("meta")
        y_biased = sem("y_biased")
        y_ready = sem("y_ready")
        added = sem("added")
        dve_chain = sem("dve_chain")

        block = ctx.enter_context(nc.Block())

        N_SMALL = 18
        N_CONSTS = 9

        def tile_loop(eng, step):
            for s in range(PEEL):
                step(s, s)
            with eng.Fori(PEEL, MAXT, UNROLL) as s:
                for u in range(UNROLL):
                    step(s + u, PEEL + u)
            for s in range(MAXT, MAXT + STAGES - 1):
                step(s, s)

        def exists(s, lag):
            return not isinstance(s, int) or 0 <= s - lag < MAXT

        def later(s, tile):
            return not isinstance(s, int) or s >= tile

        @block.sync
        def _(sp):
            def load_pair(n):
                if n >= 2:
                    sp.wait_ge(rotated, n - 1)
                sp.dma_start(xin[:, n % 2], x_pairs[n]).then_inc(x_in[n % 2], 16)

            load_pair(0)
            load_pair(1)
            sp.wait_ge(pad_ready, 2)
            sp.dma_start(sent[E * CAP:E * CAP + P, :], pad_row[:]).then_inc(pads_fixed, 16)
            sp.dma_start(out[N:N + P, :], pad_row[:, 0:D]).then_inc(pads_fixed, 16)
            for n in range(PAIRS):
                sp.wait_ge(rotated, n + 1)
                sp.dma_start(out_pairs[n], xr[:, n % 3]).then_inc(x_out[n % 3], 16)
                if n + 2 < PAIRS:
                    load_pair(n + 2)

            for half in range(2):
                sp.wait_ge(rows_sent[half], 16 * TOPK * PT * GROUPS)
            sp.wait_ge(pads_first, 16)
            sp.wait_ge(pads_fixed, 32)
            sp.wait_ge(table_ready, 1)

            def step(s, u):
                if not exists(s, 0):
                    return
                i = u % UNROLL
                if later(s, UNROLL):
                    sp.wait_ge(hin_t, s - (UNROLL - 1))
                    sp.wait_ge(meta, s - (UNROLL - 1))
                base = sp.value_load(table[0:1, T_BASE, bass.ds(s, 1)], min_val=0, max_val=E * CAP)
                sp.dma_start(got[:, i, :], sent[bass.ds(base, P), :]).then_inc(got_in[i], 16)

            step(0, 0)
            sp.wait_ge(pads_rest, 16 * (E - 1))
            for s in range(1, PEEL):
                step(s, s)
            with sp.Fori(PEEL, MAXT, UNROLL) as s:
                for u in range(UNROLL):
                    step(s + u, PEEL + u)
            sp.wait_ge(added, 16 * MAXT)

        @block.gpsimd
        def _(pool):
            def load_expert(e):
                pool.dma_start(stage[:, 0:DC * FF].rearrange("p (c f) -> p c f", c=DC),
                               exp_w1[e].rearrange("(c p) f -> p c f", p=P)).then_inc(stage_in, 16)
                pool.dma_start(stage[:, DC * FF:WE].rearrange("p (c d) -> p c d", c=FC),
                               exp_w2[e].rearrange("(c p) d -> p c d", p=P)).then_inc(stage_in, 16)
                pool.dma_start(stage[:, WE:WE + FF], exp_b1[e].partition_broadcast(P)).then_inc(stage_in, 16)
                pool.dma_start(stage[:, WE + FF:], exp_b2[e].partition_broadcast(P)).then_inc(stage_in, 16)

            def split_expert(slot, n):
                w = wts[:, slot * 2 * WE:(slot + 1) * 2 * WE]
                pool.wait_ge(stage_in, (n + 1) * 64)
                nc.gpsimd.tensor_copy(w[:, 0:WE], stage[:, 0:WE]).then_inc(w_high, 1)
                nc.gpsimd.tensor_copy(bias[:, slot * BE:(slot + 1) * BE], stage[:, WE:])
                pool.wait_ge(w_high, n + 1)
                nc.gpsimd.tensor_tensor(w[:, WE:], stage[:, 0:WE], w[:, 0:WE],
                                        ALU.subtract).then_inc(w_ready, 1)
                pool.wait_ge(w_ready, n + 1)

            nc.gpsimd.memset(ident[:], 1.0)
            nc.gpsimd.memset(before[:], 1.0)
            nc.gpsimd.memset(upto[:], 1.0)
            nc.gpsimd.memset(ones[:], 1.0)
            nc.gpsimd.memset(pad_row[:], 0.0).then_inc(consts, 1)
            pool.wait_ge(consts, 1)
            nc.gpsimd.affine_select(out=ident[:], in_=ident[:], compare_op=ALU.is_equal, fill=0.0, base=0,
                                    pattern=[[-1, P]], channel_multiplier=1).then_inc(consts, 1)
            nc.gpsimd.affine_select(out=before[:], in_=before[:], compare_op=ALU.is_gt, fill=0.0, base=0,
                                    pattern=[[1, P]], channel_multiplier=-1).then_inc(consts, 1)
            nc.gpsimd.iota(iota_p[:], pattern=[[0, 1]], base=0, channel_multiplier=1,
                           allow_small_or_imprecise_dtypes=True).then_inc(consts, 1)
            nc.gpsimd.iota(pad_row[:, D + E:ROW], pattern=[[0, 1]], base=N, channel_multiplier=1,
                           allow_small_or_imprecise_dtypes=True).then_inc(pad_ready, 2)
            nc.gpsimd.affine_select(out=upto[:], in_=upto[:], compare_op=ALU.is_ge, fill=0.0, base=0,
                                    pattern=[[1, E], [-1, E]], channel_multiplier=0).then_inc(consts, 1)
            nc.gpsimd.iota(rev[:], pattern=[[-1, E]], base=E, channel_multiplier=0,
                           allow_small_or_imprecise_dtypes=True).then_inc(consts, 1)
            nc.gpsimd.iota(ebase[:], pattern=[[CAP, E]], base=0, channel_multiplier=0,
                           allow_small_or_imprecise_dtypes=True)
            nc.gpsimd.iota(carry[:], pattern=[[CAP, E]], base=0, channel_multiplier=0,
                           allow_small_or_imprecise_dtypes=True).then_inc(consts, 1)
            nc.gpsimd.iota(tok[:], pattern=[[P, GT]], base=0, channel_multiplier=1,
                           allow_small_or_imprecise_dtypes=True).then_inc(consts, 1)
            nc.gpsimd.iota(tiles[:], pattern=[[1, MAXT]], base=0, channel_multiplier=0,
                           allow_small_or_imprecise_dtypes=True)
            nc.gpsimd.iota(thresholds[:], pattern=[[P, N // P]], base=0, channel_multiplier=0,
                           allow_small_or_imprecise_dtypes=True).then_inc(consts, 1)
            load_expert(0)
            split_expert(0, 0)
            load_expert(1)

            for g in range(GROUPS):
                pool.wait_ge(slots_ready, g + 1)
                for half in range(2):
                    pool.wait_ge(rows_filled, 2 * g + half + 1)
                    for i in range(half * PT, (half + 1) * PT):
                        for k in range(TOPK):
                            nc.gpsimd.indirect_dma_start(
                                out=sent, out_offset=bass.IndirectOffsetOnAxis(ap=slot_u[:, k, i:i + 1], axis=0),
                                in_=rows[:, i, :], in_offset=None).then_inc(rows_sent[half], 16)
            pool.wait_ge(pad_idx, 1)
            pool.wait_ge(pad_ready, 2)
            for e in range(E):
                nc.gpsimd.indirect_dma_start(
                    out=sent, out_offset=bass.IndirectOffsetOnAxis(ap=pad_u[:, e:e + 1], axis=0),
                    in_=pad_row[:], in_offset=None).then_inc(pads_first if e == 0 else pads_rest, 16)

            for i in range(3):
                pool.wait_ge(x_out[i], 16 * len(range(i, PAIRS, 3)))
            pool.wait_ge(pads_fixed, 32)
            pool.wait_ge(table_ready, 1)

            def step(s, u):
                if not exists(s, STAGES - 1):
                    return
                t = s - (STAGES - 1)
                i = (u - (STAGES - 1)) % UNROLL
                split = pool.value_load(table[0:1, T_SPLIT, bass.ds(t, 1)], min_val=0, max_val=1)
                with pool.If(split > 0):
                    e = pool.value_load(table[0:1, T_EXPERT, bass.ds(t, 1)], min_val=0, max_val=E - 1)
                    other = pool.value_load(table[0:1, T_OTHER, bass.ds(t, 1)], min_val=0, max_val=1)
                    more = pool.value_load(table[0:1, T_LOAD, bass.ds(t, 1)], min_val=0, max_val=E - 1)
                    pool.wait_ge(stage_in, (e + 2) * 64)
                    nc.gpsimd.tensor_copy(wts[:, bass.ds(other * (2 * WE), WE)], stage[:, 0:WE]).then_inc(w_high, 1)
                    nc.gpsimd.tensor_copy(bias[:, bass.ds(other * BE, BE)], stage[:, WE:])
                    pool.wait_ge(w_high, e + 2)
                    nc.gpsimd.tensor_tensor(wts[:, bass.ds(other * (2 * WE) + WE, WE)], stage[:, 0:WE],
                                            wts[:, bass.ds(other * (2 * WE), WE)],
                                            ALU.subtract).then_inc(w_ready, 1)
                    with pool.If(more > 0):
                        pool.wait_ge(w_ready, e + 2)
                        pool.wait_ge(table_ready, 1)
                        load_expert(more)
                pool.wait_ge(pads_fixed, 32)
                if later(s, STAGES):
                    pool.wait_ge(added, 16 * t if isinstance(s, int) else adds)
                pool.wait_ge(y_ready, t + 1 if isinstance(s, int) else outputs)
                nc.gpsimd.indirect_dma_start(
                    out=out, out_offset=bass.IndirectOffsetOnAxis(ap=dest[:, i:i + 1], axis=0),
                    in_=y[:, i, :], in_offset=None, compute_op=ALU.add).then_inc(added, 16)
                if not isinstance(s, int):
                    pool.reg_add(outputs, outputs, 1)
                    pool.reg_add(adds, adds, 16)

            outputs, adds = pool.alloc_register("outputs"), pool.alloc_register("adds")
            pool.reg_mov(outputs, PEEL - (STAGES - 1) + 1)
            pool.reg_mov(adds, 16 * (PEEL - (STAGES - 1)))
            tile_loop(pool, step)
            pool.wait_ge(added, 16 * MAXT)

        @block.scalar
        def _(act):
            for dst, src in (
                (th[:, 0, :], theta.partition_broadcast(P)),
                (th[:, 1, :], phi.partition_broadcast(P)),
                (ids_i[:], itok.partition_broadcast(SUBJ)),
                (emb[:], subj_emb),
                (hw1[:], hyp_w1),
                (hb1[:], hyp_b1.rearrange("(p a) -> p a", a=1)),
                (hw2[:], hyp_w2),
                (hb2[:], hyp_b2.rearrange("(p a) -> p a", a=1)),
                (sw1[:], sty_w1),
                (sb1[:], sty_b1.rearrange("(p a) -> p a", a=1)),
                (sw2[:], sty_w2),
                (rw[:], router_w.rearrange("(c p) e -> p c e", p=P)),
            ):
                act.dma_start(dst, src).then_inc(small_in, 16)
            with nc.allow_non_contiguous_dma(reason="small per-feature columns"):
                for c in range(DC):
                    act.dma_start(g_c[:, c:c + 1], ln_g.rearrange("(c p a) -> c p a", p=P, a=1)[c]).then_inc(small_in, 16)
                    act.dma_start(b_c[:, c:c + 1], ln_b.rearrange("(c p a) -> c p a", p=P, a=1)[c]).then_inc(small_in, 16)
                act.dma_start(sb2[:], sty_b2.rearrange("(c p) -> p c", p=P)).then_inc(small_in, 16)
            act.wait_ge(angle, 1)
            nc.scalar.activation(sn[:], red[:], ACT.Sin).then_inc(trig, 1)
            nc.scalar.activation(cs[:], co_arg[:], ACT.Sin).then_inc(trig, 1)
            act.wait_ge(trig, 2)

            def products(n):
                act.wait_ge(x_in[n % 2], 16 * (n // 2 + 1))
                if n >= 3:
                    act.wait_ge(x_out[n % 3], 16 * (n // 3))
                    act.wait_ge(normed, n - 2)
                for j in range(2):
                    b = 2 * n + j
                    src = xin[:, n % 2, 2 * j:2 * j + 2, :].rearrange("p i (g a r) -> p (i g) a r", a=2, r=2)
                    dst = xr[:, n % 3, 2 * j:2 * j + 2, :].rearrange("p i (g a r) -> p (i g) a r", a=2, r=2)
                    for a in range(2):
                        last = nc.scalar.mul(dst[:, :, a, :], src[:, :, a, :], cs[:, a, b:b + 1])
                last.then_inc(scaled, 1)

            def apply_norm(n):
                act.wait_ge(coefs, n + 1)
                if n >= 2:
                    act.wait_ge(turned_back, n - 1)
                for j in range(2):
                    for c in range(DC):
                        k = j * DC + c
                        last = nc.scalar.activation(h_t[:, n % 2, c, j * S:(j + 1) * S],
                                                    zt_ps[n % 2][:, j, c * S:(c + 1) * S], ACT.Identity,
                                                    bias=co_b[:, n % 2, k:k + 1], scale=co_a[:, n % 2, k:k + 1])
                last.then_inc(h_ready, 1)

            def fill_rows(n):
                act.wait_ge(turned_back, n + 1)
                if n >= 2:
                    act.wait_ge(rows_sent[n % 2], 16 * TOPK * PT * (n // 2))
                nc.scalar.copy(rows[:, (n % 2) * PT:(n % 2 + 1) * PT, 0:D],
                               back_ps.rearrange("p j (i d) -> p (j i) d", d=D)).then_inc(rows_filled, 1)

            def gate_exp(g):
                act.wait_ge(dm_ready, g + 1)
                nc.scalar.activation(ex[:], dm[:], ACT.Exp).then_inc(ex_ready, 1)

            def inverse_root(which, n):
                act.wait_ge(var_ready[which], n + 1)
                nc.scalar.activation(log_v[:, which, :], var_e[:, which, :], ACT.Ln).then_inc(log_ready[which], 1)
                act.wait_ge(log_ready[which], n + 1)
                nc.scalar.activation(rs0[:, which, :], log_v[:, which, :], ACT.Exp,
                                     scale=-0.5).then_inc(rs0_ready[which], 1)

            products(0)
            products(1)
            act.wait_ge(soft_in, 1)
            nc.scalar.activation(soft[:, 1], soft[:, 0], ACT.Exp, scale=-1.0).then_inc(soft_ex, 1)
            act.wait_ge(soft_p1, 1)
            nc.scalar.activation(soft[:, 2], soft[:, 1], ACT.Ln).then_inc(soft_ln, 1)
            inverse_root(0, 0)
            inverse_root(0, 1)
            products(2)
            inverse_root(1, 0)
            apply_norm(0)
            fill_rows(0)
            for n in range(2, PAIRS):
                inverse_root(0, n)
                if n + 1 < PAIRS:
                    products(n + 1)
                if n % 2 == 1:
                    gate_exp((n - 3) // 2)
                inverse_root(1, n - 1)
                apply_norm(n - 1)
                fill_rows(n - 1)
            inverse_root(1, PAIRS - 1)
            apply_norm(PAIRS - 1)
            fill_rows(PAIRS - 1)
            gate_exp(GROUPS - 1)

            def step(s, u):
                if exists(s, 0):
                    i = u % 2
                    act.wait_ge(hin_t, s + 1)
                    if later(s, 2):
                        act.wait_ge(l1_done, s - 1)
                    nc.scalar.copy(hin_hi[:, i, :], hin_ps).then_inc(hin_high, 1)
                if exists(s, 2):
                    t, i = s - 2, (u - 2) % 2
                    act.wait_ge(hidt_done, t + 1)
                    if later(s, 4):
                        act.wait_ge(l2_done, t - 1)
                    nc.scalar.activation(hid_hi[:, i, :].rearrange("p (k n) -> p k n", k=2), hidt_ps,
                                         ACT.Relu).then_inc(hid_high, 1)
                if exists(s, 3):
                    t, i = s - 3, (u - 3) % UNROLL
                    act.wait_ge(y_biased, t + 1)
                    if later(s, 3 + UNROLL):
                        act.wait_ge(added, 16 * (t - (UNROLL - 1)))
                    nc.scalar.mul(y[:, i, :], y_raw[:, i, :], gate[:, i:i + 1]).then_inc(y_ready, 1)

            tile_loop(act, step)

        @block.vector
        def _(dve):
            links = [0]

            def link(ins):
                links[0] += 1
                ins.then_inc(dve_chain, 1)
                dve.wait_ge(dve_chain, links[0])

            dve.wait_ge(small_in, 16 * 17)
            link(nc.vector.tensor_scalar(turns_i[:], th[:], 1.0 / (TWO_PI_A + TWO_PI_B), None, ALU.mult))
            link(nc.vector.tensor_copy(turns[:], turns_i[:]))
            link(nc.vector.scalar_tensor_tensor(red[:], turns[:], -TWO_PI_A, th[:], ALU.mult, ALU.add))
            link(nc.vector.scalar_tensor_tensor(red[:], turns[:], -TWO_PI_B, red[:], ALU.mult, ALU.add))
            link(nc.vector.scalar_tensor_tensor(co_arg[:], red[:], -1.0, red[:], ALU.mult, ALU.max))
            nc.vector.tensor_scalar(co_arg[:], co_arg[:], -1.0, HALF_PI, ALU.mult, ALU.add).then_inc(angle, 1)

            dve.wait_ge(consts, N_CONSTS)
            link(nc.vector.tensor_copy(ids[:], ids_i[:]))
            nc.vector.tensor_scalar(onehot[:], ids[:], iota_p[0:SUBJ, :], None, ALU.is_equal).then_inc(style_sb, 1)
            for j in range(2):
                nc.vector.tensor_copy(g4[:, j, :], g_c[:])
                last = nc.vector.tensor_copy(b4[:, j, :], b_c[:])
            link(last)
            nc.vector.tensor_tensor(gg4[:], g4[:], g4[:], ALU.mult)
            link(nc.vector.tensor_scalar(thresholds[:, 0:1], thresholds[:, 0:1], -1.0, None, ALU.add))
            dve.wait_ge(trig, 2)
            link(nc.vector.tensor_scalar(nsn[:], sn[:], -1.0, None, ALU.mult))
            dve.wait_ge(style_mm, 1)
            nc.vector.tensor_copy(se_t[:], style_ps[0:SE, 0:B]).then_inc(style_sb, 1)
            dve.wait_ge(style_mm, 2)
            nc.vector.tensor_scalar(hyp1[:], style_ps[:, B:2 * B], hb1[:], 0.0, ALU.add, ALU.max).then_inc(style_sb, 1)
            dve.wait_ge(style_mm, 3)
            nc.vector.tensor_scalar(hyp2[:], style_ps[:, 2 * B:3 * B], hb2[:], None, ALU.add).then_inc(style_sb, 1)
            dve.wait_ge(style_mm, 4)
            nc.vector.tensor_scalar(sty1[:], style_ps[0:SH // 2, 3 * B:4 * B], sb1[:], 0.0, ALU.add,
                                    ALU.max).then_inc(style_sb, 1)
            dve.wait_ge(style_mm, 5)
            link(nc.vector.tensor_tensor(sty[:], style_ps[:, 4 * B:8 * B].rearrange("p (c b) -> p c b", b=B),
                                         sb2[:, :, None].to_broadcast([P, 2 * DC, B]), ALU.add))
            nc.vector.tensor_copy(beta[:].rearrange("p b c -> p c b"), sty[:, DC:, :])
            nc.vector.scalar_tensor_tensor(soft[:, 0], sty[:, 0:DC, :], -1.0, sty[:, 0:DC, :], ALU.mult,
                                           ALU.max).then_inc(soft_in, 1)
            dve.wait_ge(soft_ex, 1)
            nc.vector.tensor_scalar(soft[:, 1], soft[:, 1], 1.0, None, ALU.add).then_inc(soft_p1, 1)
            dve.wait_ge(soft_ln, 1)
            link(nc.vector.scalar_tensor_tensor(soft[:, 2], sty[:, 0:DC, :], 0.0, soft[:, 2], ALU.max, ALU.add))
            link(nc.vector.tensor_scalar(gamma[:].rearrange("p b c -> p c b"), soft[:, 2], SOFTPLUS_EPS, None,
                                         ALU.add))

            def rotate(n):
                xi, xo = xin[:, n % 2], xr[:, n % 3]
                dve.wait_ge(scaled, n + 1)
                for j in range(2):
                    b = 2 * n + j
                    vi = xi[:, 2 * j:2 * j + 2, :].rearrange("p i (g r) -> p (i g) r", r=4)
                    vo = xo[:, 2 * j:2 * j + 2, :].rearrange("p i (g r) -> p (i g) r", r=4)
                    for r in range(4):
                        s = (sn if r % 2 == 0 else nsn)[:, r // 2, b:b + 1]
                        last = nc.vector.scalar_tensor_tensor(vo[:, :, r], vi[:, :, r ^ 1], s, vo[:, :, r],
                                                              ALU.mult, ALU.add)
                last.then_inc(rotated, 1)
                dve.wait_ge(rotated, n + 1)
                for i in range(PT):
                    last = nc.vector.bn_stats(st[:, i, :], xo[:, i, :])
                link(last)
                for i in range(PT):
                    last = nc.vector.bn_aggr(mv[:, i, :], st[:, i, :])
                link(last)
                nc.vector.tensor_scalar(var_e[:, 0, :], mv[:, :, 1], LN_EPS, None, ALU.add).then_inc(var_ready[0], 1)

            def newton(which, n, rs):
                dve.wait_ge(rs0_ready[which], n + 1)
                r0 = rs0[:, which, :]
                link(nc.vector.tensor_tensor(sq[:], r0, r0, ALU.mult))
                link(nc.vector.tensor_tensor(sq[:], sq[:], var_e[:, which, :], ALU.mult))
                link(nc.vector.tensor_scalar(sq[:], sq[:], -0.5, 1.5, ALU.mult, ALU.add))
                link(nc.vector.tensor_tensor(rs[:], sq[:], r0, ALU.mult))

            def normalise(n):
                xo = xr[:, n % 3]
                newton(0, n, rstd)
                if n >= 2:
                    dve.wait_ge(turned, n - 1)
                for i in range(PT):
                    last = nc.vector.tensor_scalar(z[:, n % 2, i, :], xo[:, i, :], mv[:, i, 0:1], rstd[:, i:i + 1],
                                                   ALU.subtract, ALU.mult)
                last.then_inc(normed, 1)

            def time_stats(n):
                dve.wait_ge(turned, n + 1)
                for j in range(2):
                    for c in range(DC):
                        last = nc.vector.bn_stats(st_t[:, j * DC + c, :], zt_ps[n % 2][:, j, c * S:(c + 1) * S])
                link(last)
                for k in range(2 * DC):
                    last = nc.vector.bn_aggr(mv_t[:, k, :], st_t[:, k, :])
                link(last)
                g, b, gg = (v[:].rearrange("p j c -> p (j c)") for v in (g4, b4, gg4))
                mean = tmp4[:, 0, :]
                link(nc.vector.tensor_tensor(tmp4[:, 1, :], mv_t[:, :, 1], gg, ALU.mult))
                nc.vector.tensor_scalar(var_e[:, 1, :], tmp4[:, 1, :], IN_EPS, None, ALU.add).then_inc(var_ready[1], 1)
                link(nc.vector.tensor_tensor(mean, mv_t[:, :, 0], g, ALU.mult))
                link(nc.vector.tensor_tensor(mean, mean, b, ALU.add))
                link(nc.vector.tensor_tensor(tmp4[:, 2, :], b, mean, ALU.subtract))

            def time_coefs(n):
                newton(1, n, rs_t)
                g = g4[:].rearrange("p j c -> p (j c)")
                ga = gamma[:, 2 * n:2 * n + 2, :].rearrange("p b c -> p (b c)")
                be = beta[:, 2 * n:2 * n + 2, :].rearrange("p b c -> p (b c)")
                scale = tmp4[:, 3, :]
                link(nc.vector.tensor_tensor(scale, rs_t[:], ga, ALU.mult))
                nc.vector.tensor_tensor(co_a[:, n % 2, :], scale, g, ALU.mult)
                link(nc.vector.tensor_tensor(tmp4[:, 4, :], tmp4[:, 2, :], scale, ALU.mult))
                nc.vector.tensor_tensor(co_b[:, n % 2, :], tmp4[:, 4, :], be, ALU.add).then_inc(coefs, 1)

            def over_tiles(v):
                return v[:, None, :].to_broadcast([P, GT, E])

            def over_experts(v):
                return v[:, :, None].to_broadcast([P, GT, E])

            def best(src, mx, at, oh):
                link(nc.vector.tensor_reduce(mx[:], src[:], AX_X, ALU.max))
                link(nc.vector.tensor_tensor(pick[:], src[:], over_experts(mx), ALU.is_equal))
                link(nc.vector.tensor_tensor(pick[:], pick[:], over_tiles(rev), ALU.mult))
                link(nc.vector.tensor_reduce(at[:], pick[:], AX_X, ALU.max))
                link(nc.vector.tensor_tensor(oh[:], over_tiles(rev), over_experts(at), ALU.is_equal))

            def route(g):
                dve.wait_ge(turned_back, 2 * g + 2)
                nc.vector.tensor_copy(lg[:].rearrange("p i e -> p (i e)"), logit_ps).then_inc(logits_read, 1)
                dve.wait_ge(logits_read, g + 1)
                best(lg, mx1, at1, oh1)
                link(nc.vector.scalar_tensor_tensor(lg2[:], oh1[:], FAR, lg[:], ALU.mult, ALU.add))
                best(lg2, mx2, at2, oh2)
                nc.vector.tensor_tensor(dm[:], mx2[:], mx1[:], ALU.subtract).then_inc(dm_ready, 1)
                if g >= 1:
                    dve.wait_ge(ranks, g)
                nc.vector.tensor_tensor(mask[:], oh1[:], oh2[:], ALU.add).then_inc(mask_ready, 1)
                if g >= 1:
                    for half in range(2):
                        dve.wait_ge(rows_sent[half], 16 * TOPK * PT * g)
                nc.vector.tensor_copy(rows[:, :, D + E], tok[:])
                dve.wait_ge(ranks, g + 1)
                link(nc.vector.tensor_tensor(place[:], rank_ps[:, 0:GT, :], over_tiles(carry), ALU.add))
                nc.vector.tensor_tensor(pick[:], place[:], oh1[:], ALU.mult)
                link(nc.vector.tensor_tensor(lg2[:], place[:], oh2[:], ALU.mult))
                nc.vector.tensor_reduce(slot_f[:, 0, :], pick[:], AX_X, ALU.add)
                link(nc.vector.tensor_reduce(slot_f[:, 1, :], lg2[:], AX_X, ALU.add))
                nc.vector.tensor_copy(slot_u[:], slot_f[:])
                nc.vector.tensor_tensor(carry[:], carry[:], rank_ps[:, GT, :], ALU.add)
                nc.vector.tensor_scalar(tok[:], tok[:], float(GT * P), None, ALU.add)
                dve.wait_ge(ex_ready, g + 1)
                link(nc.vector.tensor_scalar(den[:], ex[:], 1.0, None, ALU.add))
                link(nc.vector.reciprocal(gate1[:], den[:]))
                link(nc.vector.tensor_tensor(gate2[:], ex[:], gate1[:], ALU.mult))
                nc.vector.tensor_tensor(comb1[:], oh1[:], over_experts(gate1), ALU.mult)
                link(nc.vector.tensor_tensor(comb2[:], oh2[:], over_experts(gate2), ALU.mult))
                nc.vector.tensor_tensor(rows[:, :, D:D + E], comb1[:], comb2[:], ALU.add).then_inc(slots_ready, 1)

            rotate(0)
            normalise(0)
            rotate(1)
            normalise(1)
            time_stats(0)
            time_coefs(0)
            for n in range(2, PAIRS):
                rotate(n)
                if n % 2 == 1:
                    route((n - 3) // 2)
                time_stats(n - 1)
                normalise(n)
                time_coefs(n - 1)
            time_stats(PAIRS - 1)
            time_coefs(PAIRS - 1)
            route(GROUPS - 1)

            dve.wait_ge(slots_ready, GROUPS)
            link(nc.vector.tensor_scalar(pad_f[:], carry[:], iota_p[:], None, ALU.add))
            nc.vector.tensor_copy(pad_u[:], pad_f[:]).then_inc(pad_idx, 1)
            link(nc.vector.tensor_tensor(cnt[:], carry[0:1, :], ebase[0:1, :], ALU.subtract))
            link(nc.vector.tensor_tensor(over[:], cnt[:, :, None].to_broadcast([1, E, N // P]),
                                         thresholds[:, None, :].to_broadcast([1, E, N // P]), ALU.is_gt))
            link(nc.vector.tensor_reduce(n_t[:], over[:], AX_X, ALU.add))
            link(nc.vector.tensor_tensor(cum[:], upto[:], n_t[:, None, :].to_broadcast([1, E, E]), ALU.mult))
            link(nc.vector.tensor_reduce(end[:], cum[:], AX_X, ALU.add))
            link(nc.vector.tensor_tensor(past[:], tiles[:, :, None].to_broadcast([1, MAXT, E]),
                                         end[:, None, :].to_broadcast([1, MAXT, E]), ALU.is_ge))
            link(nc.vector.tensor_tensor(pastn[:], past[:], n_t[:, None, :].to_broadcast([1, MAXT, E]), ALU.mult))
            nc.vector.tensor_reduce(done_e[:], past[:], AX_X, ALU.add)
            link(nc.vector.tensor_reduce(start_t[:], pastn[:], AX_X, ALU.add))
            f = [tf[:, k, :] for k in range(9)]
            nc.vector.tensor_scalar(f[T_EXPERT], done_e[:], float(E - 1), None, ALU.min)
            link(nc.vector.tensor_tensor(f[7], tiles[:], start_t[:], ALU.subtract))
            nc.vector.tensor_scalar(f[T_NEED], f[T_EXPERT], 1.0, None, ALU.add)
            nc.vector.tensor_scalar(f[T_BASE], done_e[:], float(CAP), None, ALU.mult)
            nc.vector.tensor_scalar(f[8], done_e[:], float(E - 1), None, ALU.is_lt)
            nc.vector.tensor_scalar(f[T_LOAD], done_e[:], float(E - 2), None, ALU.is_lt)
            nc.vector.tensor_copy(f[T_SLOT], f[T_EXPERT])
            link(nc.vector.tensor_scalar(f[T_OTHER], f[T_EXPERT], 1.0, None, ALU.add))
            nc.vector.scalar_tensor_tensor(f[T_BASE], f[7], float(P), f[T_BASE], ALU.mult, ALU.add)
            link(nc.vector.scalar_tensor_tensor(f[T_SPLIT], f[7], 0.0, f[8], ALU.is_equal, ALU.mult))
            nc.vector.tensor_scalar(f[T_BASE], f[T_BASE], float(E * CAP), None, ALU.min)
            nc.vector.tensor_scalar(f[8], f[T_EXPERT], 2.0, None, ALU.add)
            link(nc.vector.tensor_tensor(f[T_LOAD], f[T_LOAD], f[T_SPLIT], ALU.mult))
            link(nc.vector.tensor_tensor(f[T_LOAD], f[T_LOAD], f[8], ALU.mult))
            link(nc.vector.tensor_copy(table[:, :, 0:MAXT], tf[:, 0:7, :]))
            nc.vector.tensor_scalar(table[:, T_SLOT, 0:MAXT], table[:, T_SLOT, 0:MAXT], 1, None,
                                    ALU.bitwise_and)
            nc.vector.tensor_scalar(table[:, T_OTHER, 0:MAXT], table[:, T_OTHER, 0:MAXT], 1, None,
                                    ALU.bitwise_and).then_inc(table_ready, 1)
            dve.wait_ge(table_ready, 1)

            def step(s, u):
                if exists(s, 0):
                    i = u % 2
                    dve.wait_ge(hin_high, s + 1)
                    nc.vector.tensor_tensor(hin_lo[:, i, :], hin_ps, hin_hi[:, i, :], ALU.subtract).then_inc(hin_low, 1)
                if exists(s, 1):
                    t, i = s - 1, (u - 1) % 2
                    slot = dve.value_load(table[0:1, T_SLOT, bass.ds(t, 1)], min_val=0, max_val=1)
                    dve.wait_ge(l1_done, t + 1)
                    if later(s, 3):
                        dve.wait_ge(hidt_done, t - 1)
                    nc.vector.tensor_tensor(hid[:, i, :].rearrange("p (k n) -> p k n", k=2), hid_ps,
                                            bias[:, bass.ds(slot * BE, FF)].rearrange("p (k n) -> p k n", k=2),
                                            ALU.add).then_inc(hid_biased, 1)
                if exists(s, 2):
                    t, i, k = s - 2, (u - 2) % 2, (u - 2) % UNROLL
                    e = dve.value_load(table[0:1, T_EXPERT, bass.ds(t, 1)], min_val=0, max_val=E - 1)
                    if later(s, 2 + UNROLL):
                        dve.wait_ge(added, 16 * (t - (UNROLL - 1)))
                    nc.vector.tensor_copy(gate[:, k:k + 1], got[:, k, bass.ds(e + D, 1)])
                    nc.vector.tensor_copy(dest[:, k:k + 1], got[:, k, D + E:ROW]).then_inc(meta, 1)
                    dve.wait_ge(hid_high, t + 1)
                    nc.vector.scalar_tensor_tensor(hid_lo[:, i, :].rearrange("p (k n) -> p k n", k=2), hidt_ps, 0.0,
                                                   hid_hi[:, i, :].rearrange("p (k n) -> p k n", k=2),
                                                   ALU.max, ALU.subtract).then_inc(hid_low, 1)
                if exists(s, 3):
                    t, i = s - 3, (u - 3) % UNROLL
                    slot = dve.value_load(table[0:1, T_SLOT, bass.ds(t, 1)], min_val=0, max_val=1)
                    dve.wait_ge(l2_done, t + 1)
                    if later(s, 3 + UNROLL):
                        dve.wait_ge(y_ready, t - (UNROLL - 1))
                    nc.vector.tensor_tensor(y_raw[:, i, :], y_ps[(u - 3) % 2], bias[:, bass.ds(slot * BE + FF, D)],
                                            ALU.add).then_inc(y_biased, 1)

            tile_loop(dve, step)

        @block.tensor
        def _(pe):
            pe.wait_ge(small_in, 16 * 17)
            pe.wait_ge(consts, N_CONSTS)
            pe.wait_ge(style_sb, 1)
            nc.tensor.matmul(style_ps[0:SE, 0:B], emb[:], onehot[:], start=True, stop=True).then_inc(style_mm, 1)
            pe.wait_ge(style_sb, 2)
            nc.tensor.matmul(style_ps[:, B:2 * B], hw1[:], se_t[:], start=True, stop=True).then_inc(style_mm, 1)
            pe.wait_ge(style_sb, 3)
            nc.tensor.matmul(style_ps[:, 2 * B:3 * B], hw2[:], hyp1[:], start=True, stop=True).then_inc(style_mm, 1)
            pe.wait_ge(style_sb, 4)
            nc.tensor.matmul(style_ps[0:SH // 2, 3 * B:4 * B], sw1[:], hyp2[:], start=True,
                             stop=True).then_inc(style_mm, 1)
            pe.wait_ge(style_sb, 5)
            for c in range(2 * DC):
                last = nc.tensor.matmul(style_ps[:, (4 + c) * B:(5 + c) * B], sw2[:, c * P:(c + 1) * P], sty1[:],
                                        start=True, stop=True)
            last.then_inc(style_mm, 1)

            def turn(n):
                pe.wait_ge(normed, n + 1)
                if n >= 2:
                    pe.wait_ge(h_ready, n - 1)
                for i in range(PT):
                    for c in range(DC):
                        q = c * S + (i % 2) * P
                        last = nc.tensor.transpose(zt_ps[n % 2][:, i // 2, q:q + P], z[:, n % 2, i, c * P:(c + 1) * P],
                                                   ident[:])
                last.then_inc(turned, 1)

            def logits_and_back(n):
                pe.wait_ge(h_ready, n + 1)
                if n == 0:
                    pe.wait_ge(soft_in, 1)
                if n % 2 == 0 and n >= 2:
                    pe.wait_ge(logits_read, n // 2)
                for i in range(PT):
                    k = (n % 2) * PT + i
                    for c in range(DC):
                        nc.tensor.matmul(logit_ps[:, k * E:(k + 1) * E], h_t[:, n % 2, c, i * P:(i + 1) * P],
                                         rw[:, c, :], start=(c == 0), stop=(c == DC - 1))
                if n >= 1:
                    pe.wait_ge(rows_filled, n)
                for i in range(PT):
                    for c in range(DC):
                        q = (i % 2) * D + c * P
                        last = nc.tensor.transpose(back_ps[:, i // 2, q:q + P], h_t[:, n % 2, c, i * P:(i + 1) * P],
                                                   ident[:])
                last.then_inc(turned_back, 1)

            def rank(g):
                pe.wait_ge(mask_ready, g + 1)
                if g >= 1:
                    pe.wait_ge(slots_ready, g)
                flat = ps[:, 7, :]
                nc.tensor.matmul(flat[:, 0:GT * E], before[:], mask[:].rearrange("p i e -> p (i e)"),
                                 start=True, stop=False, skip_group_check=True)
                for i in range(GT):
                    reps = GT - i
                    last = nc.tensor.matmul(rank_ps[:, i + 1:GT + 1, :], ones[:],
                                            mask[:, i:i + 1, :].to_broadcast([P, reps, E]),
                                            start=False, stop=(i == GT - 1), skip_group_check=True)
                last.then_inc(ranks, 1)

            turn(0)
            turn(1)
            logits_and_back(0)
            for n in range(2, PAIRS):
                if n >= 3 and n % 2 == 1:
                    rank((n - 3) // 2)
                turn(n)
                logits_and_back(n - 1)
            logits_and_back(PAIRS - 1)
            rank(GROUPS - 1)
            pe.wait_ge(slots_ready, GROUPS)
            pe.wait_ge(table_ready, 1)

            def step(s, u):
                if exists(s, 0):
                    i = u % UNROLL
                    pe.wait_ge(got_in[i], 16 * (s // UNROLL + 1) if isinstance(s, int)
                               else ((s - i) * (16 // UNROLL) + 16))
                    if later(s, 1):
                        pe.wait_ge(hin_low, s)
                    for c in range(DC):
                        last = nc.tensor.transpose(hin_ps[:, c * P:(c + 1) * P], got[:, i, c * P:(c + 1) * P], ident[:])
                    last.then_inc(hin_t, 1)
                if exists(s, 1):
                    t, i = s - 1, (u - 1) % 2
                    slot = pe.value_load(table[0:1, T_SLOT, bass.ds(t, 1)], min_val=0, max_val=1)
                    need = pe.value_load(table[0:1, T_NEED, bass.ds(t, 1)], min_val=1, max_val=E)
                    pe.wait_ge(w_ready, need)
                    pe.wait_ge(hin_low, t + 1)
                    if later(s, 2):
                        pe.wait_ge(hid_biased, t)
                    for c in range(DC):
                        for part, against in ((hin_hi, (0, 1)), (hin_lo, (0,))):
                            for w in against:
                                for k in range(FF // NB):
                                    first = c == 0 and part is hin_hi and w == 0
                                    stop = c == DC - 1 and part is hin_lo
                                    off = slot * (2 * WE) + (w * WE + c * FF + k * NB)
                                    last = nc.tensor.matmul(hid_ps[:, k, :], part[:, i, c * P:(c + 1) * P],
                                                            wts[:, bass.ds(off, NB)], start=first, stop=stop)
                    last.then_inc(l1_done, 1)
                if exists(s, 2):
                    t, i = s - 2, (u - 2) % 2
                    pe.wait_ge(hid_biased, t + 1)
                    if later(s, 3):
                        pe.wait_ge(hid_low, t)
                    for k in range(FC):
                        last = nc.tensor.transpose(hidt_ps[:, k // 4, (k % 4) * P:(k % 4 + 1) * P],
                                                   hid[:, i, k * P:(k + 1) * P], ident[:])
                    last.then_inc(hidt_done, 1)
                if exists(s, 3):
                    t, i = s - 3, (u - 3) % 2
                    slot = pe.value_load(table[0:1, T_SLOT, bass.ds(t, 1)], min_val=0, max_val=1)
                    pe.wait_ge(hid_low, t + 1)
                    if later(s, 5):
                        pe.wait_ge(y_biased, t - 1)
                    for k in range(FC):
                        for part, against in ((hid_hi, (0, 1)), (hid_lo, (0,))):
                            for w in against:
                                off = slot * (2 * WE) + (w * WE + DC * FF + k * D)
                                last = nc.tensor.matmul(y_ps[i], part[:, i, k * P:(k + 1) * P],
                                                        wts[:, bass.ds(off, D)],
                                                        start=(k == 0 and part is hid_hi and w == 0),
                                                        stop=(k == FC - 1 and part is hid_lo))
                    last.then_inc(l2_done, 1)

            tile_loop(pe, step)


_INS = ['x', 'condB_theta', 'condB_phi', 'itok_B_6_14', 'L1_cond_ln_g', 'L1_cond_ln_b', 'L1_cond_subj_emb',
        'L1_cond_hyp_w1', 'L1_cond_hyp_b1', 'L1_cond_hyp_w2', 'L1_cond_hyp_b2', 'L1_cond_sty_w1', 'L1_cond_sty_b1',
        'L1_cond_sty_w2', 'L1_cond_sty_b2', 'L1_cond_router_w', 'L1_cond_exp_w1', 'L1_cond_exp_b1',
        'L1_cond_exp_w2', 'L1_cond_exp_b2']


def kernel(**inputs):
    import numpy as _np
    import concourse.bacc as _bacc
    from concourse import mybir as _mybir
    from concourse.bass_utils import run_bass_kernel_spmd as _run

    nc = _bacc.Bacc("TRN2", target_bir_lowering=False, num_devices=1)
    arrays, args = {}, []
    for name in _INS:
        a = _np.ascontiguousarray(inputs[name])
        arrays[f"in_{name}_dram"] = a
        args.append(nc.dram_tensor(f"in_{name}_dram", a.shape, _mybir.dt.from_np(a.dtype), kind="ExternalInput").ap())
    args.append(nc.dram_tensor("out_0_dram", (N + P, D), F32, kind="ExternalOutput").ap())
    moe_kernel(nc, *args)
    r = _run(nc, [arrays], core_ids=[0])
    return r.results[0]["out_0_dram"][0:N].reshape(B, S, D)
```

```python
from contextlib import ExitStack

import concourse.bass as bass
from concourse import mybir

ALU = mybir.AluOpType
ACT = mybir.ActivationFunctionType
AX_X = mybir.AxisListType.X
F32 = mybir.dt.float32
F32R = mybir.dt.float32r
BF16 = mybir.dt.bfloat16
I32 = mybir.dt.int32
U32 = mybir.dt.uint32

P = 128
B, S, D = 16, 256, 256
N = B * S
E, FF, TOPK = 8, 1024, 2
SUBJ, SE, SH = 32, 64, 128
DC = D // P
FC = FF // P
PAIRS = B // 2
PT = 2 * S // P
GROUPS = PAIRS // 2
GT = 2 * PT
ET = 2 * P
ETB = ET // P
CAP = N + ET
ROW = D + E + 1
MAXT = N * TOPK // ET + E - 1
UNROLL = 4
STAGES = 3
PEEL = STAGES + UNROLL
WE = DC * FF + FC * D
NB = 512
HB = FF * ET // P // NB
LN_EPS, IN_EPS, SOFTPLUS_EPS = 1e-5, 1e-8, 1e-8
TWO_PI_A, TWO_PI_B = 6.28125, 0.0019353071795864769
HALF_PI = 1.5707963267948966
FAR = -3.0e38
T_EXPERT, T_NEED, T_SLOT, T_BASE, T_SPLIT, T_LOAD, T_OTHER = range(7)
assert (MAXT - PEEL) % UNROLL == 0


def moe_kernel(nc, x, theta, phi, itok, ln_g, ln_b, subj_emb, hyp_w1, hyp_b1, hyp_w2, hyp_b2,
               sty_w1, sty_b1, sty_w2, sty_b2, router_w, exp_w1, exp_b1, exp_w2, exp_b2, out):
    sent = nc.dram_tensor("sent_rows", (E * CAP + ET, ROW), F32).ap()
    def sent_tile(row):
        return sent[bass.ds(row, ET), :].rearrange("(r p) d -> p r d", p=P)

    x_pairs = x.rearrange("(n j) (i p) d -> n p (j i) d", j=2, p=P)
    out_pairs = out[0:N, :].rearrange("(n i p) d -> n p i d", i=PT, p=P)

    with ExitStack() as ctx:
        def sb(name, shape, dt=F32):
            return ctx.enter_context(nc.sbuf_tensor(name, shape, dt))

        def sem(name):
            return ctx.enter_context(nc.semaphore(name))

        ident = sb("ident", [P, P])
        before = sb("before", [P, P], BF16)
        ones = sb("ones", [P, P], BF16)
        iota_p = sb("iota_p", [P, 1])
        rev = sb("rev", [P, E])
        ebase = sb("ebase", [P, E])
        tok = sb("tok", [P, GT])
        pad_rows = sb("pad_rows", [P, ETB, ROW])
        thresholds = sb("thresholds", [1, N // ET])
        upto = sb("upto", [1, E, E])
        tiles = sb("tiles", [1, MAXT])
        th = sb("th", [P, 2, B])
        g_c = sb("g_c", [P, DC])
        b_c = sb("b_c", [P, DC])
        rw = sb("rw", [P, DC, E])
        ids_i = sb("ids_i", [SUBJ, B], I32)
        ids = sb("ids", [SUBJ, B])
        onehot = sb("onehot", [SUBJ, B])
        emb = sb("emb", [SUBJ, SE])
        hw1 = sb("hw1", [SE, SH])
        hw2 = sb("hw2", [SH, SH])
        sw1 = sb("sw1", [SH, SH // 2])
        sw2 = sb("sw2", [SH // 2, 2 * D])
        hb1 = sb("hb1", [SH, 1])
        hb2 = sb("hb2", [SH, 1])
        sb1 = sb("sb1", [SH // 2, 1])
        sb2 = sb("sb2", [P, 2 * DC])
        se_t = sb("se_t", [SE, B])
        hyp1 = sb("hyp1", [SH, B])
        hyp2 = sb("hyp2", [SH, B])
        sty1 = sb("sty1", [SH // 2, B])
        sty = sb("sty", [P, 2 * DC, B])
        soft = sb("soft", [P, 3, DC, B])
        gamma = sb("gamma", [P, B, DC])
        beta = sb("beta", [P, B, DC])
        turns_i = sb("turns_i", [P, 2, B], I32)
        turns = sb("turns", [P, 2, B])
        red = sb("red", [P, 2, B])
        co_arg = sb("co_arg", [P, 2, B])
        sn = sb("sn", [P, 2, B])
        cs = sb("cs", [P, 2, B])
        nsn = sb("nsn", [P, 2, B])
        xr = sb("xr", [P, 3, PT, D])
        st = sb("st", [P, PT, 6])
        mv = sb("mv", [P, PT, 2])
        var_e = sb("var_e", [P, 2, 2 * DC])
        log_v = sb("log_v", [P, 2, 2 * DC])
        rs0 = sb("rs0", [P, 2, 2 * DC])
        sq = sb("sq", [P, 2, 2 * DC])
        rs = sb("rs", [P, 2, 2 * DC])
        st_t = sb("st_t", [P, 2 * DC, 6])
        mv_t = sb("mv_t", [P, 2 * DC, 2])
        g4 = sb("g4", [P, 2, DC])
        b4 = sb("b4", [P, 2, DC])
        gg4 = sb("gg4", [P, 2, DC])
        tmp4 = sb("tmp4", [P, 6, 2 * DC])
        co_a = sb("co_a", [P, 2, 2 * DC])
        co_b = sb("co_b", [P, 2, 2 * DC])
        rows = sb("rows", [P, GT, ROW])
        lg = sb("lg", [P, GT, E])
        lg2 = sb("lg2", [P, GT, E])
        pick = sb("pick", [P, GT, E])
        oh1 = sb("oh1", [P, GT, E])
        oh2 = sb("oh2", [P, GT, E])
        mask = sb("mask", [P, GT, E], BF16)
        mx1 = sb("mx1", [P, GT])
        mx2 = sb("mx2", [P, GT])
        at1 = sb("at1", [P, GT])
        at2 = sb("at2", [P, GT])
        dm = sb("dm", [P, GT])
        ex = sb("ex", [P, GT])
        den = sb("den", [P, GT])
        gate1 = sb("gate1", [P, GT])
        gate2 = sb("gate2", [P, GT])
        comb1 = sb("comb1", [P, GT, E])
        comb2 = sb("comb2", [P, GT, E])
        place = sb("place", [P, GT, E])
        slot_f = sb("slot_f", [P, TOPK, GT])
        slot_u = sb("slot_u", [P, TOPK, GT], U32)
        carry = sb("carry", [P, E])
        pad_at = sb("pad_at", [1, E], I32)
        cnt = sb("cnt", [1, E])
        over = sb("over", [1, E, N // ET])
        n_t = sb("n_t", [1, E])
        cum = sb("cum", [1, E, E])
        end = sb("end", [1, E])
        past = sb("past", [1, MAXT, E])
        pastn = sb("pastn", [1, MAXT, E])
        done_e = sb("done_e", [1, MAXT])
        start_t = sb("start_t", [1, MAXT])
        tf = sb("tf", [1, 9, MAXT])
        table = sb("table", [1, 7, MAXT + UNROLL], I32)
        b1_rows = sb("b1_rows", [E * FC, P])
        b1_all = sb("b1_all", [P, E * FC])
        b2_all = sb("b2_all", [P, E * D])
        stage = sb("stage", [P, WE])
        wts = sb("wts", [P, 2 * 2 * WE], F32R)
        got = sb("got", [P, UNROLL, ETB, ROW])
        gate = sb("gate", [P, UNROLL, ETB])
        dest = sb("dest", [P, UNROLL, ETB], U32)
        b1 = sb("b1", [P, 2, FC])
        hin_hi = sb("hin_hi", [P, 2, DC * ET], F32R)
        hin_lo = sb("hin_lo", [P, 2, DC * ET], F32R)
        hid = sb("hid", [P, FC * ET])
        y_raw = sb("y_raw", [P, 2, ETB, D])
        y = sb("y", [P, 2, ETB, D])

        with ExitStack() as early:
            def sb_early(name, shape, dt=F32):
                return early.enter_context(nc.sbuf_tensor(name, shape, dt))

            xin = sb_early("xin", [P, 2, PT, D])
            z = sb_early("z", [P, 2, PT, D])
            h_t = sb_early("h_t", [P, 2, DC, PT * P])
        hid_hi = sb("hid_hi", [P, 2, FC * ET], F32R)
        hid_lo = sb("hid_lo", [P, 2, FC * ET], F32R)

        ps = ctx.enter_context(nc.psum_tensor("ps", [P, 8, NB], F32))
        zt_ps = [ps[:, 0:2, :], ps[:, 2:4, :]]
        back_ps = ps[:, 4:6, :]
        logit_ps = ps[:, 6, 0:GT * E]
        rank_ps = ps[:, 7, 0:(GT + 1) * E].rearrange("p (i e) -> p i e", e=E)
        style_ps = ps[:, 5, :]
        b1_ps = ps[:, 5, NB // 2:NB // 2 + E * FC]
        hin_ps = [ps[:, 0, :], ps[:, 1, :]]
        hid_ps = ps[:, 2:2 + HB, :]
        y_ps = [ps[:, 6, :], ps[:, 7, :]]

        angles_in = sem("angles_in")
        small_in = sem("small_in")
        x_in = [sem("x_in0"), sem("x_in1")]
        consts = sem("consts")
        pad_ready = sem("pad_ready")
        angle = sem("angle")
        trig = sem("trig")
        style_mm = sem("style_mm")
        style_sb = sem("style_sb")
        soft_in = sem("soft_in")
        soft_ex = sem("soft_ex")
        soft_p1 = sem("soft_p1")
        soft_ln = sem("soft_ln")
        scaled = sem("scaled")
        rotated = sem("rotated")
        x_out = [sem("x_out0"), sem("x_out1"), sem("x_out2")]
        var_ready = sem("var_ready")
        log_ready = sem("log_ready")
        rs0_ready = sem("rs0_ready")
        normed = sem("normed")
        turned = sem("turned")
        coefs = sem("coefs")
        h_ready = sem("h_ready")
        logits_ready = sem("logits_ready")
        turned_back = sem("turned_back")
        rows_filled = sem("rows_filled")
        logits_read = sem("logits_read")
        dm_ready = sem("dm_ready")
        ex_ready = sem("ex_ready")
        mask_ready = sem("mask_ready")
        ranks = sem("ranks")
        slots_ready = sem("slots_ready")
        rows_sent = [sem("rows_sent0"), sem("rows_sent1")]
        pad_idx = sem("pad_idx")
        pads_in = sem("pads_in")
        pads_fixed = sem("pads_fixed")
        table_ready = sem("table_ready")
        stage_in = sem("stage_in")
        w_high = sem("w_high")
        w_ready = sem("w_ready")
        got_in = [sem(f"got_in{i}") for i in range(UNROLL)]
        hin_t = sem("hin_t")
        hin_high = sem("hin_high")
        hin_low = sem("hin_low")
        l1_done = sem("l1_done")
        hid_read = sem("hid_read")
        hid_high = sem("hid_high")
        hid_low = sem("hid_low")
        l2_done = sem("l2_done")
        meta = sem("meta")
        y_biased = sem("y_biased")
        y_ready = sem("y_ready")
        added = sem("added")
        dve_chain = sem("dve_chain")

        block = ctx.enter_context(nc.Block())

        N_SMALL = 15
        N_CONSTS = 9

        def tile_loop(eng, step):
            for s in range(PEEL):
                step(s, s)
            with eng.Fori(PEEL, MAXT, UNROLL) as s:
                for u in range(UNROLL):
                    step(s + u, PEEL + u)
            for s in range(MAXT, MAXT + STAGES - 1):
                step(s, s)

        def exists(s, lag):
            return not isinstance(s, int) or 0 <= s - lag < MAXT

        def later(s, tile):
            return not isinstance(s, int) or s >= tile

        @block.sync
        def _(sp):
            def load_pair(n):
                if n >= 2:
                    sp.wait_ge(rotated, n - 1)
                sp.dma_start(xin[:, n % 2], x_pairs[n]).then_inc(x_in[n % 2], 16)

            sp.dma_start(th[:, 0, :], theta.partition_broadcast(P)).then_inc(angles_in, 16)
            sp.dma_start(th[:, 1, :], phi.partition_broadcast(P)).then_inc(angles_in, 16)
            load_pair(0)
            load_pair(1)
            with nc.allow_non_contiguous_dma(reason="small per-feature columns"):
                for dst, src in (
                    (sw2[:], sty_w2),
                    (sb2[:], sty_b2.rearrange("(c p) -> p c", p=P)),
                    (g_c[:], ln_g.rearrange("(c p) -> p c", p=P)),
                    (b_c[:], ln_b.rearrange("(c p) -> p c", p=P)),
                    (rw[:], router_w.rearrange("(c p) e -> p c e", p=P)),
                    (b1_rows[:], exp_b1.rearrange("e (k p) -> (e k) p", p=P)),
                    (b2_all[:], exp_b2.rearrange("e d -> (e d)").partition_broadcast(P)),
                ):
                    sp.dma_start(dst, src).then_inc(small_in, 16)
            sp.wait_ge(pad_ready, 2)
            sp.dma_start(sent_tile(E * CAP), pad_rows[:]).then_inc(pads_fixed, 16)
            sp.dma_start(out[N:N + ET, :].rearrange("(r p) d -> p r d", p=P), pad_rows[:, :, 0:D]).then_inc(pads_fixed, 16)
            for n in range(PAIRS):
                sp.wait_ge(rotated, n + 1)
                sp.dma_start(out_pairs[n], xr[:, n % 3]).then_inc(x_out[n % 3], 16)
                if n + 2 < PAIRS:
                    load_pair(n + 2)

            sp.wait_ge(pad_idx, 1)
            for e in range(E):
                row = sp.value_load(pad_at[0:1, e:e + 1], min_val=e * CAP, max_val=e * CAP + N)
                sp.dma_start(sent_tile(row), pad_rows[:]).then_inc(pads_in, 16)

            sp.wait_ge(table_ready, 1)
            sp.wait_ge(pads_in, 16 * E)
            sp.wait_ge(pads_fixed, 32)
            for half in range(2):
                sp.wait_ge(rows_sent[half], 16 * TOPK * PT * GROUPS)

            def step(s, u):
                if not exists(s, 0):
                    return
                i = u % UNROLL
                if later(s, UNROLL):
                    sp.wait_ge(hin_t, s - (UNROLL - 1))
                    sp.wait_ge(meta, s - (UNROLL - 1))
                base = sp.value_load(table[0:1, T_BASE, bass.ds(s, 1)], min_val=0, max_val=E * CAP)
                sp.dma_start(got[:, i], sent_tile(base)).then_inc(got_in[i], 16)

            tile_loop(sp, step)
            sp.wait_ge(added, 16 * ETB * MAXT)

        @block.gpsimd
        def _(pool):
            def load_expert(e):
                pool.dma_start(stage[:, 0:DC * FF].rearrange("p (c f) -> p c f", c=DC),
                               exp_w1[e].rearrange("(c p) f -> p c f", p=P)).then_inc(stage_in, 16)
                pool.dma_start(stage[:, DC * FF:WE].rearrange("p (c d) -> p c d", c=FC),
                               exp_w2[e].rearrange("(c p) d -> p c d", p=P)).then_inc(stage_in, 16)

            load_expert(0)
            nc.gpsimd.memset(ident[:], 1.0)
            nc.gpsimd.memset(before[:], 1.0)
            nc.gpsimd.memset(upto[:], 1.0)
            nc.gpsimd.memset(ones[:], 1.0)
            nc.gpsimd.memset(pad_rows[:], 0.0).then_inc(consts, 1)
            pool.wait_ge(consts, 1)
            nc.gpsimd.affine_select(out=ident[:], in_=ident[:], compare_op=ALU.is_equal, fill=0.0, base=0,
                                    pattern=[[-1, P]], channel_multiplier=1).then_inc(consts, 1)
            nc.gpsimd.affine_select(out=before[:], in_=before[:], compare_op=ALU.is_gt, fill=0.0, base=0,
                                    pattern=[[1, P]], channel_multiplier=-1).then_inc(consts, 1)
            nc.gpsimd.iota(iota_p[:], pattern=[[0, 1]], base=0, channel_multiplier=1,
                           allow_small_or_imprecise_dtypes=True).then_inc(consts, 1)
            nc.gpsimd.iota(pad_rows[:, :, D + E], pattern=[[P, ETB]], base=N, channel_multiplier=1,
                           allow_small_or_imprecise_dtypes=True).then_inc(pad_ready, 2)
            nc.gpsimd.affine_select(out=upto[:], in_=upto[:], compare_op=ALU.is_ge, fill=0.0, base=0,
                                    pattern=[[1, E], [-1, E]], channel_multiplier=0).then_inc(consts, 1)
            nc.gpsimd.iota(rev[:], pattern=[[-1, E]], base=E, channel_multiplier=0,
                           allow_small_or_imprecise_dtypes=True).then_inc(consts, 1)
            nc.gpsimd.iota(ebase[:], pattern=[[CAP, E]], base=0, channel_multiplier=0,
                           allow_small_or_imprecise_dtypes=True)
            nc.gpsimd.iota(carry[:], pattern=[[CAP, E]], base=0, channel_multiplier=0,
                           allow_small_or_imprecise_dtypes=True).then_inc(consts, 1)
            nc.gpsimd.iota(tok[:], pattern=[[P, GT]], base=0, channel_multiplier=1,
                           allow_small_or_imprecise_dtypes=True).then_inc(consts, 1)
            nc.gpsimd.iota(tiles[:], pattern=[[1, MAXT]], base=0, channel_multiplier=0,
                           allow_small_or_imprecise_dtypes=True)
            nc.gpsimd.iota(thresholds[:], pattern=[[ET, N // ET]], base=0, channel_multiplier=0,
                           allow_small_or_imprecise_dtypes=True).then_inc(consts, 1)
            pool.wait_ge(w_high, 1)
            nc.gpsimd.tensor_tensor(wts[:, WE:2 * WE], stage[:], wts[:, 0:WE], ALU.subtract).then_inc(w_ready, 1)
            pool.wait_ge(w_ready, 1)
            load_expert(1)

            for g in range(GROUPS):
                pool.wait_ge(slots_ready, g + 1)
                for half in range(2):
                    pool.wait_ge(rows_filled, 2 * g + half + 1)
                    for i in range(half * PT, (half + 1) * PT):
                        for k in range(TOPK):
                            nc.gpsimd.indirect_dma_start(
                                out=sent, out_offset=bass.IndirectOffsetOnAxis(ap=slot_u[:, k, i:i + 1], axis=0),
                                in_=rows[:, i, :], in_offset=None).then_inc(rows_sent[half], 16)
            for i in range(3):
                pool.wait_ge(x_out[i], 16 * len(range(i, PAIRS, 3)))
            pool.wait_ge(pads_fixed, 32)
            pool.wait_ge(table_ready, 1)

            def step(s, u):
                if not exists(s, STAGES - 1):
                    return
                t = s - (STAGES - 1)
                i = (u - (STAGES - 1)) % UNROLL
                pool.wait_ge(pads_fixed, 32)
                if later(s, STAGES):
                    pool.wait_ge(added, 16 * ETB * t if isinstance(s, int) else adds)
                pool.wait_ge(y_ready, t + 1 if isinstance(s, int) else outputs)
                for r in range(ETB):
                    nc.gpsimd.indirect_dma_start(
                        out=out, out_offset=bass.IndirectOffsetOnAxis(ap=dest[:, i, r:r + 1], axis=0),
                        in_=y[:, i % 2, r, :], in_offset=None, compute_op=ALU.add).then_inc(added, 16)
                if not isinstance(s, int):
                    pool.reg_add(outputs, outputs, 1)
                    pool.reg_add(adds, adds, 16 * ETB)
                split = pool.value_load(table[0:1, T_SPLIT, bass.ds(t, 1)], min_val=0, max_val=1)
                with pool.If(split > 0):
                    e = pool.value_load(table[0:1, T_EXPERT, bass.ds(t, 1)], min_val=0, max_val=E - 1)
                    other = pool.value_load(table[0:1, T_OTHER, bass.ds(t, 1)], min_val=0, max_val=1)
                    more = pool.value_load(table[0:1, T_LOAD, bass.ds(t, 1)], min_val=0, max_val=E - 1)
                    pool.wait_ge(w_high, e + 2)
                    nc.gpsimd.tensor_tensor(wts[:, bass.ds(other * (2 * WE) + WE, WE)], stage[:],
                                            wts[:, bass.ds(other * (2 * WE), WE)],
                                            ALU.subtract).then_inc(w_ready, 1)
                    with pool.If(more > 0):
                        pool.wait_ge(w_ready, e + 2)
                        load_expert(more)

            outputs, adds = pool.alloc_register("outputs"), pool.alloc_register("adds")
            pool.reg_mov(outputs, PEEL - (STAGES - 1) + 1)
            pool.reg_mov(adds, 16 * ETB * (PEEL - (STAGES - 1)))
            tile_loop(pool, step)
            pool.wait_ge(added, 16 * ETB * MAXT)

        @block.scalar
        def _(act):
            nc.scalar.preload_act_table_set("trig_and_small")
            for dst, src in (
                (ids_i[:], itok.partition_broadcast(SUBJ)),
                (emb[:], subj_emb),
                (hw1[:], hyp_w1),
                (hb1[:], hyp_b1.rearrange("(p a) -> p a", a=1)),
                (hw2[:], hyp_w2),
                (hb2[:], hyp_b2.rearrange("(p a) -> p a", a=1)),
                (sw1[:], sty_w1),
                (sb1[:], sty_b1.rearrange("(p a) -> p a", a=1)),
            ):
                act.dma_start(dst, src).then_inc(small_in, 16)
            act.wait_ge(angle, 1)
            nc.scalar.activation(sn[:], red[:], ACT.Sin).then_inc(trig, 1)
            nc.scalar.activation(nsn[:], red[:], ACT.Sin, scale=-1.0).then_inc(trig, 1)
            nc.scalar.activation(cs[:], co_arg[:], ACT.Sin).then_inc(trig, 1)
            nc.scalar.preload_act_table_set("natural_log_exp_and_others")
            act.wait_ge(trig, 3)

            def products(n):
                act.wait_ge(x_in[n % 2], 16 * (n // 2 + 1))
                if n >= 2:
                    act.wait_ge(turned, n - 1)
                if n >= 3:
                    act.wait_ge(x_out[n % 3], 16 * (n // 3))
                    act.wait_ge(normed, n - 2)
                for j in range(2):
                    b = 2 * n + j
                    src, dst, swp = (v[:, 2 * j:2 * j + 2, :].rearrange("p i (g r) -> p (i g) r", r=4)
                                     for v in (xin[:, n % 2], xr[:, n % 3], z[:, n % 2]))
                    for a in range(2):
                        nc.scalar.mul(dst[:, :, 2 * a:2 * a + 2], src[:, :, 2 * a:2 * a + 2], cs[:, a, b:b + 1])
                        for k in range(2):
                            last = nc.scalar.mul(swp[:, :, 2 * a + k], src[:, :, 2 * a + 1 - k],
                                                 (sn, nsn)[k][:, a, b:b + 1])
                last.then_inc(scaled, 1)

            def apply_norm(n):
                act.wait_ge(coefs, n + 1)
                if n >= 2:
                    act.wait_ge(turned_back, n - 1)
                for j in range(2):
                    for c in range(DC):
                        k = j * DC + c
                        last = nc.scalar.activation(h_t[:, n % 2, c, j * S:(j + 1) * S],
                                                    zt_ps[n % 2][:, j, c * S:(c + 1) * S], ACT.Identity,
                                                    bias=co_b[:, n % 2, k:k + 1], scale=co_a[:, n % 2, k:k + 1])
                last.then_inc(h_ready, 1)

            def fill_rows(n):
                act.wait_ge(turned_back, n + 1)
                if n >= 2:
                    act.wait_ge(rows_sent[n % 2], 16 * TOPK * PT * (n // 2))
                nc.scalar.copy(rows[:, (n % 2) * PT:(n % 2 + 1) * PT, 0:D],
                               back_ps.rearrange("p j (i d) -> p (j i) d", d=D)).then_inc(rows_filled, 1)

            def gate_exp(g):
                act.wait_ge(dm_ready, g + 1)
                nc.scalar.activation(ex[:], dm[:], ACT.Exp).then_inc(ex_ready, 1)

            def inverse_roots(n):
                act.wait_ge(var_ready, n + 1)
                nc.scalar.activation(log_v[:], var_e[:], ACT.Ln).then_inc(log_ready, 1)
                act.wait_ge(log_ready, n + 1)
                nc.scalar.activation(rs0[:], log_v[:], ACT.Exp, scale=-0.5).then_inc(rs0_ready, 1)

            products(0)
            products(1)
            inverse_roots(0)
            act.wait_ge(stage_in, 32)
            nc.scalar.copy(wts[:, 0:WE], stage[:]).then_inc(w_high, 1)
            inverse_roots(1)
            products(2)
            act.wait_ge(soft_in, 1)
            nc.scalar.activation(soft[:, 1], soft[:, 0], ACT.Exp, scale=-1.0).then_inc(soft_ex, 1)
            act.wait_ge(soft_p1, 1)
            nc.scalar.activation(soft[:, 2], soft[:, 1], ACT.Ln).then_inc(soft_ln, 1)
            apply_norm(0)
            fill_rows(0)
            for n in range(2, PAIRS + 1):
                inverse_roots(n)
                if n % 2 == 1:
                    gate_exp((n - 3) // 2)
                if n + 1 < PAIRS:
                    products(n + 1)
                apply_norm(n - 1)
                fill_rows(n - 1)
            gate_exp(GROUPS - 1)

            def step(s, u):
                if exists(s, 0):
                    i = u % 2
                    act.wait_ge(hin_t, s + 1)
                    if later(s, 2):
                        act.wait_ge(l1_done, (s - 1) * HB)
                    nc.scalar.copy(hin_hi[:, i, :], hin_ps[i]).then_inc(hin_high, 1)
                if exists(s, 1):
                    t, i = s - 1, (u - 1) % 2
                    act.wait_ge(meta, t + 1)
                    for k in range(FC):
                        if later(s, 2) and k % (FC // 2) == 0:
                            act.wait_ge(hid_low, (t - 1) * 2 + (k // (FC // 2) + 1))
                        if k % 2 == 0:
                            act.wait_ge(l1_done, t * HB + (k // 2 + 1))
                        last = nc.scalar.activation(hid[:, k * ET:(k + 1) * ET],
                                                    hid_ps[:, k // 2, (k % 2) * ET:(k % 2 + 1) * ET], ACT.Relu,
                                                    bias=b1[:, i, k:k + 1])
                        if k % 2 == 1:
                            last.then_inc(hid_read, 1)
                if exists(s, 2):
                    t, i = s - 2, (u - 2) % UNROLL
                    act.wait_ge(y_biased, t + 1)
                    if later(s, 4):
                        act.wait_ge(added, (t - 1) * (16 * ETB))
                    for r in range(ETB):
                        last = nc.scalar.mul(y[:, i % 2, r, :], y_raw[:, i % 2, r, :], gate[:, i, r:r + 1])
                    last.then_inc(y_ready, 1)
                    split = act.value_load(table[0:1, T_SPLIT, bass.ds(t, 1)], min_val=0, max_val=1)
                    with act.If(split > 0):
                        e = act.value_load(table[0:1, T_EXPERT, bass.ds(t, 1)], min_val=0, max_val=E - 1)
                        other = act.value_load(table[0:1, T_OTHER, bass.ds(t, 1)], min_val=0, max_val=1)
                        act.wait_ge(stage_in, (e + 2) * 32)
                        nc.scalar.copy(wts[:, bass.ds(other * (2 * WE), WE)], stage[:]).then_inc(w_high, 1)

            act.wait_ge(table_ready, 1)
            tile_loop(act, step)

        @block.vector
        def _(dve):
            links = [0]

            def link(ins):
                links[0] += 1
                ins.then_inc(dve_chain, 1)
                dve.wait_ge(dve_chain, links[0])

            link(nc.vector.memset(var_e[:], 1.0))
            dve.wait_ge(angles_in, 32)
            link(nc.vector.tensor_scalar(turns_i[:], th[:], 1.0 / (TWO_PI_A + TWO_PI_B), None, ALU.mult))
            link(nc.vector.tensor_copy(turns[:], turns_i[:]))
            link(nc.vector.scalar_tensor_tensor(red[:], turns[:], -TWO_PI_A, th[:], ALU.mult, ALU.add))
            link(nc.vector.scalar_tensor_tensor(red[:], turns[:], -TWO_PI_B, red[:], ALU.mult, ALU.add))
            link(nc.vector.scalar_tensor_tensor(co_arg[:], red[:], -1.0, red[:], ALU.mult, ALU.max))
            nc.vector.tensor_scalar(co_arg[:], co_arg[:], -1.0, HALF_PI, ALU.mult, ALU.add).then_inc(angle, 1)

            def style_start():
                dve.wait_ge(small_in, 16 * N_SMALL)
                dve.wait_ge(consts, N_CONSTS)
                link(nc.vector.tensor_copy(ids[:], ids_i[:]))
                nc.vector.tensor_scalar(onehot[:], ids[:], iota_p[0:SUBJ, :], None, ALU.is_equal).then_inc(style_sb, 1)
                for j in range(2):
                    nc.vector.tensor_copy(g4[:, j, :], g_c[:])
                    last = nc.vector.tensor_copy(b4[:, j, :], b_c[:])
                link(last)
                nc.vector.tensor_tensor(gg4[:], g4[:], g4[:], ALU.mult)

            def style_embedding():
                dve.wait_ge(style_mm, 1)
                nc.vector.tensor_copy(se_t[:], style_ps[0:SE, 0:B]).then_inc(style_sb, 1)

            def style_hyper1():
                dve.wait_ge(style_mm, 2)
                nc.vector.tensor_scalar(hyp1[:], style_ps[:, B:2 * B], hb1[:], 0.0, ALU.add, ALU.max).then_inc(style_sb, 1)

            def style_hyper2():
                dve.wait_ge(style_mm, 3)
                nc.vector.tensor_scalar(hyp2[:], style_ps[:, 2 * B:3 * B], hb2[:], None, ALU.add).then_inc(style_sb, 1)

            def style_hidden():
                dve.wait_ge(style_mm, 4)
                nc.vector.tensor_scalar(sty1[:], style_ps[0:SH // 2, 3 * B:4 * B], sb1[:], 0.0, ALU.add,
                                        ALU.max).then_inc(style_sb, 1)

            def style_out():
                dve.wait_ge(style_mm, 5)
                link(nc.vector.tensor_tensor(sty[:], style_ps[:, 4 * B:8 * B].rearrange("p (c b) -> p c b", b=B),
                                             sb2[:, :, None].to_broadcast([P, 2 * DC, B]), ALU.add))
                nc.vector.tensor_copy(b1_all[:], b1_ps)
                nc.vector.tensor_copy(beta[:].rearrange("p b c -> p c b"), sty[:, DC:, :])
                nc.vector.scalar_tensor_tensor(soft[:, 0], sty[:, 0:DC, :], -1.0, sty[:, 0:DC, :], ALU.mult,
                                               ALU.max).then_inc(soft_in, 1)

            def style_softplus():
                dve.wait_ge(soft_ex, 1)
                nc.vector.tensor_scalar(soft[:, 1], soft[:, 1], 1.0, None, ALU.add).then_inc(soft_p1, 1)
                dve.wait_ge(soft_ln, 1)
                link(nc.vector.scalar_tensor_tensor(soft[:, 2], sty[:, 0:DC, :], 0.0, soft[:, 2], ALU.max, ALU.add))
                link(nc.vector.tensor_scalar(gamma[:].rearrange("p b c -> p c b"), soft[:, 2], SOFTPLUS_EPS, None,
                                             ALU.add))

            def rotate(n):
                xo = xr[:, n % 3].rearrange("p i d -> p (i d)")
                dve.wait_ge(scaled, n + 1)
                nc.vector.tensor_tensor(xo, xo, z[:, n % 2].rearrange("p i d -> p (i d)"), ALU.add).then_inc(rotated, 1)
                dve.wait_ge(rotated, n + 1)

            def token_stats(n):
                for i in range(PT):
                    last = nc.vector.bn_stats(st[:, i, :], xr[:, n % 3, i, :])
                link(last)
                for i in range(PT):
                    last = nc.vector.bn_aggr(mv[:, i, :], st[:, i, :])
                link(last)
                return nc.vector.tensor_scalar(var_e[:, 0, :], mv[:, :, 1], LN_EPS, None, ALU.add)

            def newton(n):
                dve.wait_ge(rs0_ready, n + 1)
                link(nc.vector.tensor_tensor(sq[:], rs0[:], rs0[:], ALU.mult))
                link(nc.vector.scalar_tensor_tensor(sq[:], sq[:], -0.5, var_e[:], ALU.mult, ALU.mult))
                link(nc.vector.scalar_tensor_tensor(rs[:], sq[:], 1.5, rs0[:], ALU.add, ALU.mult))

            def normalise(n):
                for i in range(PT):
                    last = nc.vector.tensor_scalar(z[:, n % 2, i, :], xr[:, n % 3, i, :], mv[:, i, 0:1], rs[:, 0, i:i + 1],
                                                   ALU.subtract, ALU.mult)
                last.then_inc(normed, 1)

            def time_stats(n):
                dve.wait_ge(turned, n + 1)
                for j in range(2):
                    for c in range(DC):
                        last = nc.vector.bn_stats(st_t[:, j * DC + c, :], zt_ps[n % 2][:, j, c * S:(c + 1) * S])
                link(last)
                for k in range(2 * DC):
                    last = nc.vector.bn_aggr(mv_t[:, k, :], st_t[:, k, :])
                link(last)
                g, b, gg = (v[:].rearrange("p j c -> p (j c)") for v in (g4, b4, gg4))
                mean = tmp4[:, 0, :]
                link(nc.vector.tensor_tensor(tmp4[:, 1, :], mv_t[:, :, 1], gg, ALU.mult))
                nc.vector.tensor_scalar(var_e[:, 1, :], tmp4[:, 1, :], IN_EPS, None, ALU.add).then_inc(var_ready, 1)
                link(nc.vector.tensor_tensor(mean, mv_t[:, :, 0], g, ALU.mult))
                link(nc.vector.tensor_tensor(mean, mean, b, ALU.add))
                link(nc.vector.tensor_tensor(tmp4[:, 2, :], b, mean, ALU.subtract))

            def time_coefs(n):
                g = g4[:].rearrange("p j c -> p (j c)")
                ga = gamma[:, 2 * n:2 * n + 2, :].rearrange("p b c -> p (b c)")
                be = beta[:, 2 * n:2 * n + 2, :].rearrange("p b c -> p (b c)")
                scale = tmp4[:, 3, :]
                link(nc.vector.tensor_tensor(scale, rs[:, 1, :], ga, ALU.mult))
                nc.vector.tensor_tensor(co_a[:, n % 2, :], scale, g, ALU.mult)
                link(nc.vector.tensor_tensor(tmp4[:, 4, :], tmp4[:, 2, :], scale, ALU.mult))
                nc.vector.tensor_tensor(co_b[:, n % 2, :], tmp4[:, 4, :], be, ALU.add).then_inc(coefs, 1)

            def over_tiles(v):
                return v[:, None, :].to_broadcast([P, GT, E])

            def over_experts(v):
                return v[:, :, None].to_broadcast([P, GT, E])

            def best(src, mx, at, oh):
                link(nc.vector.tensor_reduce(mx[:], src[:], AX_X, ALU.max))
                link(nc.vector.tensor_tensor(pick[:], src[:], over_experts(mx), ALU.is_equal))
                link(nc.vector.tensor_tensor(pick[:], pick[:], over_tiles(rev), ALU.mult))
                link(nc.vector.tensor_reduce(at[:], pick[:], AX_X, ALU.max))
                link(nc.vector.tensor_tensor(oh[:], over_tiles(rev), over_experts(at), ALU.is_equal))

            def route(g):
                dve.wait_ge(logits_ready, 2 * g + 2)
                nc.vector.tensor_copy(lg[:].rearrange("p i e -> p (i e)"), logit_ps).then_inc(logits_read, 1)
                dve.wait_ge(logits_read, g + 1)
                best(lg, mx1, at1, oh1)
                link(nc.vector.scalar_tensor_tensor(lg2[:], oh1[:], FAR, lg[:], ALU.mult, ALU.add))
                best(lg2, mx2, at2, oh2)
                nc.vector.tensor_tensor(dm[:], mx2[:], mx1[:], ALU.subtract).then_inc(dm_ready, 1)
                if g >= 1:
                    dve.wait_ge(ranks, g)
                nc.vector.tensor_tensor(mask[:], oh1[:], oh2[:], ALU.add).then_inc(mask_ready, 1)
                if g >= 1:
                    for half in range(2):
                        dve.wait_ge(rows_sent[half], 16 * TOPK * PT * g)
                nc.vector.tensor_copy(rows[:, :, D + E], tok[:])
                dve.wait_ge(ranks, g + 1)
                link(nc.vector.tensor_tensor(place[:], rank_ps[:, 0:GT, :], over_tiles(carry), ALU.add))
                nc.vector.tensor_tensor(pick[:], place[:], oh1[:], ALU.mult)
                link(nc.vector.tensor_tensor(lg2[:], place[:], oh2[:], ALU.mult))
                nc.vector.tensor_reduce(slot_f[:, 0, :], pick[:], AX_X, ALU.add)
                link(nc.vector.tensor_reduce(slot_f[:, 1, :], lg2[:], AX_X, ALU.add))
                nc.vector.tensor_copy(slot_u[:], slot_f[:])
                nc.vector.tensor_tensor(carry[:], carry[:], rank_ps[:, GT, :], ALU.add)
                nc.vector.tensor_scalar(tok[:], tok[:], float(GT * P), None, ALU.add)
                dve.wait_ge(ex_ready, g + 1)
                link(nc.vector.tensor_scalar(den[:], ex[:], 1.0, None, ALU.add))
                link(nc.vector.reciprocal(gate1[:], den[:]))
                link(nc.vector.tensor_tensor(gate2[:], ex[:], gate1[:], ALU.mult))
                nc.vector.tensor_tensor(comb1[:], oh1[:], over_experts(gate1), ALU.mult)
                link(nc.vector.tensor_tensor(comb2[:], oh2[:], over_experts(gate2), ALU.mult))
                nc.vector.tensor_tensor(rows[:, :, D:D + E], comb1[:], comb2[:], ALU.add).then_inc(slots_ready, 1)

            rotate(0)
            token_stats(0).then_inc(var_ready, 1)
            style_start()
            newton(0)
            normalise(0)
            style_embedding()
            rotate(1)
            style_hyper1()
            token_stats(1)
            style_hyper2()
            time_stats(0)
            style_hidden()
            newton(1)
            normalise(1)
            style_out()
            rotate(2)
            style_softplus()
            time_coefs(0)
            for n in range(2, PAIRS):
                if n > 2:
                    rotate(n)
                token_stats(n)
                time_stats(n - 1)
                if n % 2 == 1:
                    route((n - 3) // 2)
                newton(n)
                time_coefs(n - 1)
                normalise(n)
            time_stats(PAIRS - 1)
            newton(PAIRS)
            time_coefs(PAIRS - 1)
            route(GROUPS - 1)

            dve.wait_ge(slots_ready, GROUPS)
            nc.vector.tensor_copy(pad_at[:], carry[0:1, :]).then_inc(pad_idx, 1)
            link(nc.vector.tensor_scalar(thresholds[:, 0:1], thresholds[:, 0:1], -1.0, None, ALU.add))
            link(nc.vector.tensor_tensor(cnt[:], carry[0:1, :], ebase[0:1, :], ALU.subtract))
            link(nc.vector.tensor_tensor(over[:], cnt[:, :, None].to_broadcast([1, E, N // ET]),
                                         thresholds[:, None, :].to_broadcast([1, E, N // ET]), ALU.is_gt))
            link(nc.vector.tensor_reduce(n_t[:], over[:], AX_X, ALU.add))
            link(nc.vector.tensor_tensor(cum[:], upto[:], n_t[:, None, :].to_broadcast([1, E, E]), ALU.mult))
            link(nc.vector.tensor_reduce(end[:], cum[:], AX_X, ALU.add))
            link(nc.vector.tensor_tensor(past[:], tiles[:, :, None].to_broadcast([1, MAXT, E]),
                                         end[:, None, :].to_broadcast([1, MAXT, E]), ALU.is_ge))
            link(nc.vector.tensor_tensor(pastn[:], past[:], n_t[:, None, :].to_broadcast([1, MAXT, E]), ALU.mult))
            nc.vector.tensor_reduce(done_e[:], past[:], AX_X, ALU.add)
            link(nc.vector.tensor_reduce(start_t[:], pastn[:], AX_X, ALU.add))
            f = [tf[:, k, :] for k in range(9)]
            nc.vector.tensor_scalar(f[T_EXPERT], done_e[:], float(E - 1), None, ALU.min)
            link(nc.vector.tensor_tensor(f[7], tiles[:], start_t[:], ALU.subtract))
            nc.vector.tensor_scalar(f[T_NEED], f[T_EXPERT], 1.0, None, ALU.add)
            nc.vector.tensor_scalar(f[T_BASE], done_e[:], float(CAP), None, ALU.mult)
            nc.vector.tensor_scalar(f[8], done_e[:], float(E - 1), None, ALU.is_lt)
            nc.vector.tensor_scalar(f[T_LOAD], done_e[:], float(E - 2), None, ALU.is_lt)
            nc.vector.tensor_copy(f[T_SLOT], f[T_EXPERT])
            link(nc.vector.tensor_scalar(f[T_OTHER], f[T_EXPERT], 1.0, None, ALU.add))
            nc.vector.scalar_tensor_tensor(f[T_BASE], f[7], float(ET), f[T_BASE], ALU.mult, ALU.add)
            link(nc.vector.scalar_tensor_tensor(f[T_SPLIT], f[7], 0.0, f[8], ALU.is_equal, ALU.mult))
            nc.vector.tensor_scalar(f[T_BASE], f[T_BASE], float(E * CAP), None, ALU.min)
            nc.vector.tensor_scalar(f[8], f[T_EXPERT], 2.0, None, ALU.add)
            link(nc.vector.tensor_tensor(f[T_LOAD], f[T_LOAD], f[T_SPLIT], ALU.mult))
            link(nc.vector.tensor_tensor(f[T_LOAD], f[T_LOAD], f[8], ALU.mult))
            link(nc.vector.tensor_copy(table[:, :, 0:MAXT], tf[:, 0:7, :]))
            nc.vector.tensor_scalar(table[:, T_SLOT, 0:MAXT], table[:, T_SLOT, 0:MAXT], 1, None,
                                    ALU.bitwise_and)
            nc.vector.tensor_scalar(table[:, T_OTHER, 0:MAXT], table[:, T_OTHER, 0:MAXT], 1, None,
                                    ALU.bitwise_and).then_inc(table_ready, 1)
            dve.wait_ge(table_ready, 1)

            half = FC * ET // 2

            def step(s, u):
                if exists(s, 0):
                    i = u % 2
                    dve.wait_ge(hin_high, s + 1)
                    nc.vector.tensor_tensor(hin_lo[:, i, :], hin_ps[i], hin_hi[:, i, :], ALU.subtract).then_inc(hin_low, 1)
                if exists(s, 1):
                    t, i, k = s - 1, (u - 1) % 2, (u - 1) % UNROLL
                    e = dve.value_load(table[0:1, T_EXPERT, bass.ds(t, 1)], min_val=0, max_val=E - 1)
                    dve.wait_ge(hin_t, t + 1)
                    if later(s, 1 + UNROLL):
                        dve.wait_ge(added, (t - (UNROLL - 1)) * (16 * ETB))
                    nc.vector.tensor_copy(b1[:, i, :], b1_all[:, bass.ds(e * FC, FC)])
                    nc.vector.tensor_copy(gate[:, k, :], got[:, k, :, bass.ds(e + D, 1)])
                    nc.vector.tensor_copy(dest[:, k, :], got[:, k, :, D + E]).then_inc(meta, 1)
                    if later(s, 3):
                        dve.wait_ge(l2_done, t - 1)
                    for h in range(2):
                        cols = slice(h * half, (h + 1) * half)
                        dve.wait_ge(hid_read, t * HB + (h + 1) * (HB // 2))
                        nc.vector.tensor_copy(hid_hi[:, i, cols], hid[:, cols]).then_inc(hid_high, 1)
                        dve.wait_ge(hid_high, t * 2 + (h + 1))
                        nc.vector.tensor_tensor(hid_lo[:, i, cols], hid[:, cols], hid_hi[:, i, cols],
                                                ALU.subtract).then_inc(hid_low, 1)
                if exists(s, 2):
                    t, i = s - 2, (u - 2) % 2
                    e = dve.value_load(table[0:1, T_EXPERT, bass.ds(t, 1)], min_val=0, max_val=E - 1)
                    dve.wait_ge(l2_done, t + 1)
                    if later(s, 4):
                        dve.wait_ge(y_ready, t - 1)
                    nc.vector.tensor_tensor(y_raw[:, i], y_ps[i].rearrange("p (r d) -> p r d", d=D),
                                            b2_all[:, None, bass.ds(e * D, D)].to_broadcast([P, ETB, D]),
                                            ALU.add).then_inc(y_biased, 1)

            tile_loop(dve, step)

        @block.tensor
        def _(pe):
            pe.wait_ge(small_in, 16 * N_SMALL)
            pe.wait_ge(consts, N_CONSTS)
            pe.wait_ge(style_sb, 1)
            nc.tensor.matmul(style_ps[0:SE, 0:B], emb[:], onehot[:], start=True, stop=True).then_inc(style_mm, 1)

            def style_rest():
                pe.wait_ge(style_sb, 2)
                nc.tensor.matmul(style_ps[:, B:2 * B], hw1[:], se_t[:], start=True, stop=True).then_inc(style_mm, 1)
                pe.wait_ge(style_sb, 3)
                nc.tensor.matmul(style_ps[:, 2 * B:3 * B], hw2[:], hyp1[:], start=True, stop=True).then_inc(style_mm, 1)
                pe.wait_ge(style_sb, 4)
                nc.tensor.transpose(b1_ps, b1_rows[:], ident[0:E * FC, 0:E * FC])
                nc.tensor.matmul(style_ps[0:SH // 2, 3 * B:4 * B], sw1[:], hyp2[:], start=True,
                                 stop=True).then_inc(style_mm, 1)
                pe.wait_ge(style_sb, 5)
                for c in range(2 * DC):
                    last = nc.tensor.matmul(style_ps[:, (4 + c) * B:(5 + c) * B], sw2[:, c * P:(c + 1) * P], sty1[:],
                                            start=True, stop=True)
                last.then_inc(style_mm, 1)

            def turn(n):
                pe.wait_ge(normed, n + 1)
                if n >= 2:
                    pe.wait_ge(h_ready, n - 1)
                for i in range(PT):
                    for c in range(DC):
                        q = c * S + (i % 2) * P
                        last = nc.tensor.transpose(zt_ps[n % 2][:, i // 2, q:q + P], z[:, n % 2, i, c * P:(c + 1) * P],
                                                   ident[:])
                last.then_inc(turned, 1)

            def logits_and_back(n):
                pe.wait_ge(h_ready, n + 1)
                if n == 0:
                    pe.wait_ge(soft_in, 1)
                if n % 2 == 0 and n >= 2:
                    pe.wait_ge(logits_read, n // 2)
                for i in range(PT):
                    k = (n % 2) * PT + i
                    for c in range(DC):
                        last = nc.tensor.matmul(logit_ps[:, k * E:(k + 1) * E], h_t[:, n % 2, c, i * P:(i + 1) * P],
                                         rw[:, c, :], start=(c == 0), stop=(c == DC - 1))
                last.then_inc(logits_ready, 1)
                if n >= 1:
                    pe.wait_ge(rows_filled, n)
                for i in range(PT):
                    for c in range(DC):
                        q = (i % 2) * D + c * P
                        last = nc.tensor.transpose(back_ps[:, i // 2, q:q + P], h_t[:, n % 2, c, i * P:(i + 1) * P],
                                                   ident[:])
                last.then_inc(turned_back, 1)

            def rank(g):
                pe.wait_ge(mask_ready, g + 1)
                if g >= 1:
                    pe.wait_ge(slots_ready, g)
                flat = ps[:, 7, :]
                nc.tensor.matmul(flat[:, 0:GT * E], before[:], mask[:].rearrange("p i e -> p (i e)"),
                                 start=True, stop=False, skip_group_check=True)
                for i in range(GT):
                    reps = GT - i
                    last = nc.tensor.matmul(rank_ps[:, i + 1:GT + 1, :], ones[:],
                                            mask[:, i:i + 1, :].to_broadcast([P, reps, E]),
                                            start=False, stop=(i == GT - 1), skip_group_check=True)
                last.then_inc(ranks, 1)

            turn(0)
            style_rest()
            turn(1)
            logits_and_back(0)
            for n in range(2, PAIRS):
                if n % 2 == 1:
                    rank((n - 3) // 2)
                turn(n)
                logits_and_back(n - 1)
            logits_and_back(PAIRS - 1)
            rank(GROUPS - 1)
            pe.wait_ge(slots_ready, GROUPS)
            pe.wait_ge(table_ready, 1)

            def step(s, u):
                if exists(s, 0):
                    i, k = u % 2, u % UNROLL
                    pe.wait_ge(got_in[k], 16 * (s // UNROLL + 1) if isinstance(s, int)
                               else ((s - k) * (16 // UNROLL) + 16))
                    if later(s, 2):
                        pe.wait_ge(hin_low, s - 1)
                    for c in range(DC):
                        for r in range(ETB):
                            last = nc.tensor.transpose(hin_ps[i][:, c * ET + r * P:c * ET + (r + 1) * P],
                                                       got[:, k, r, c * P:(c + 1) * P], ident[:])
                    last.then_inc(hin_t, 1)
                if exists(s, 1):
                    t, i = s - 1, (u - 1) % 2
                    slot = pe.value_load(table[0:1, T_SLOT, bass.ds(t, 1)], min_val=0, max_val=1)
                    need = pe.value_load(table[0:1, T_NEED, bass.ds(t, 1)], min_val=1, max_val=E)
                    pe.wait_ge(w_ready, need)
                    pe.wait_ge(hin_low, t + 1)
                    for side in range(2):
                        with pe.If(slot > 0 if side else slot < 1):
                            for k in range(FC):
                                if later(s, 2) and k % 2 == 0:
                                    pe.wait_ge(hid_read, (t - 1) * HB + (k // 2 + 1))
                                for c in range(DC):
                                    tokens = slice(c * ET, (c + 1) * ET)
                                    for w, against in ((0, (hin_hi, hin_lo)), (1, (hin_hi,))):
                                        off = side * 2 * WE + w * WE + c * FF + k * P
                                        for part in against:
                                            last = nc.tensor.matmul(hid_ps[:, k // 2, (k % 2) * ET:(k % 2 + 1) * ET],
                                                                    wts[:, off:off + P], part[:, i, tokens],
                                                                    start=(c == 0 and w == 0 and part is hin_hi),
                                                                    stop=(c == DC - 1 and w == 1))
                                if k % 2 == 1:
                                    last.then_inc(l1_done, 1)
                if exists(s, 2):
                    t, i = s - 2, (u - 2) % 2
                    slot = pe.value_load(table[0:1, T_SLOT, bass.ds(t, 1)], min_val=0, max_val=1)
                    pe.wait_ge(hid_low, (t + 1) * 2)
                    if later(s, 4):
                        pe.wait_ge(y_biased, t - 1)
                    for r in range(ETB):
                        for k in range(FC):
                            tokens = slice(k * ET + r * P, k * ET + (r + 1) * P)
                            for part, against in ((hid_hi, (0, 1)), (hid_lo, (0,))):
                                for w in against:
                                    off = slot * (2 * WE) + (w * WE + DC * FF + k * D)
                                    last = nc.tensor.matmul(y_ps[i][:, r * D:(r + 1) * D], part[:, i, tokens],
                                                            wts[:, bass.ds(off, D)],
                                                            start=(k == 0 and part is hid_hi and w == 0),
                                                            stop=(k == FC - 1 and part is hid_lo))
                    last.then_inc(l2_done, 1)

            tile_loop(pe, step)


_INS = ['x', 'condB_theta', 'condB_phi', 'itok_B_6_14', 'L1_cond_ln_g', 'L1_cond_ln_b', 'L1_cond_subj_emb',
        'L1_cond_hyp_w1', 'L1_cond_hyp_b1', 'L1_cond_hyp_w2', 'L1_cond_hyp_b2', 'L1_cond_sty_w1', 'L1_cond_sty_b1',
        'L1_cond_sty_w2', 'L1_cond_sty_b2', 'L1_cond_router_w', 'L1_cond_exp_w1', 'L1_cond_exp_b1',
        'L1_cond_exp_w2', 'L1_cond_exp_b2']


def kernel(**inputs):
    import numpy as _np
    import concourse.bacc as _bacc
    from concourse import mybir as _mybir
    from concourse.bass_utils import run_bass_kernel_spmd as _run

    nc = _bacc.Bacc("TRN2", target_bir_lowering=False, num_devices=1)
    arrays, args = {}, []
    for name in _INS:
        a = _np.ascontiguousarray(inputs[name])
        arrays[f"in_{name}_dram"] = a
        args.append(nc.dram_tensor(f"in_{name}_dram", a.shape, _mybir.dt.from_np(a.dtype), kind="ExternalInput").ap())
    args.append(nc.dram_tensor("out_0_dram", (N + 2 * P, D), F32, kind="ExternalOutput").ap())
    moe_kernel(nc, *args)
    r = _run(nc, [arrays], core_ids=[0])
    return r.results[0]["out_0_dram"][0:N].reshape(B, S, D)
```

```python
from contextlib import ExitStack, nullcontext

import concourse.bass as bass
from concourse import mybir

ALU = mybir.AluOpType
ACT = mybir.ActivationFunctionType
AX_X = mybir.AxisListType.X
F32 = mybir.dt.float32
F32R = mybir.dt.float32r
BF16 = mybir.dt.bfloat16
I32 = mybir.dt.int32
U32 = mybir.dt.uint32

P = 128
B, S, D = 16, 256, 256
N = B * S
E, FF, TOPK = 8, 1024, 2
SUBJ, SE, SH = 32, 64, 128
DC = D // P
FC = FF // P
PAIRS = B // 2
PT = 2 * S // P
GROUPS = [(n, n + 1) for n in range(0, PAIRS - 2, 2)] + [(PAIRS - 2,), (PAIRS - 1,)]
GT = 2 * PT
ET = 2 * P
ETB = ET // P
CAP = N + ET
ROW = D + E + 1
MAXT = N * TOPK // ET + E - 1
SURE = N * TOPK // ET
EARLY = (2, 2, 1)
UNROLL = 4
STAGES = 3
PEEL = STAGES + UNROLL
WE = DC * FF + FC * D
NB = 512
HB = FF * ET // P // NB
LN_EPS, IN_EPS, SOFTPLUS_EPS = 1e-5, 1e-8, 1e-8
TWO_PI_A, TWO_PI_B = 6.28125, 0.0019353071795864769
HALF_PI = 1.5707963267948966
FAR = -3.0e38
T_EXPERT, T_NEED, T_SLOT, T_BASE, T_SPLIT, T_LOAD = range(6)
assert (SURE - 1 - PEEL) % UNROLL == 0 and (MAXT - SURE + 1) % UNROLL == 0


def moe_kernel(nc, x, theta, phi, itok, ln_g, ln_b, subj_emb, hyp_w1, hyp_b1, hyp_w2, hyp_b2,
               sty_w1, sty_b1, sty_w2, sty_b2, router_w, exp_w1, exp_b1, exp_w2, exp_b2, out):
    sent = nc.dram_tensor("sent_rows", (E * CAP + ET, ROW), F32).ap()
    def sent_tile(row):
        return sent[bass.ds(row, ET), :].rearrange("(r p) d -> p r d", p=P)

    x_pairs = x.rearrange("(n j) (i p) d -> n p (j i) d", j=2, p=P)
    out_pairs = out[0:N, :].rearrange("(n i p) d -> n p i d", i=PT, p=P)

    with ExitStack() as ctx:
        def sb(name, shape, dt=F32):
            return ctx.enter_context(nc.sbuf_tensor(name, shape, dt))

        def sem(name):
            return ctx.enter_context(nc.semaphore(name))

        ident = sb("ident", [P, P])
        before = sb("before", [P, P], BF16)
        ones = sb("ones", [P, P], BF16)
        iota_p = sb("iota_p", [P, 1])
        rev = sb("rev", [P, E])
        ebase = sb("ebase", [P, E])
        tok = sb("tok", [P, GT])
        pad_rows = sb("pad_rows", [P, ETB, ROW])
        thresholds = sb("thresholds", [1, N // ET])
        upto = sb("upto", [1, E, E])
        tiles = sb("tiles", [1, MAXT])
        th = sb("th", [P, 2, B])
        g_c = sb("g_c", [P, DC])
        b_c = sb("b_c", [P, DC])
        rw = sb("rw", [P, DC, E])
        ids_i = sb("ids_i", [SUBJ, B], I32)
        ids = sb("ids", [SUBJ, B])
        onehot = sb("onehot", [SUBJ, B])
        emb = sb("emb", [SUBJ, SE])
        hw1 = sb("hw1", [SE, SH])
        hw2 = sb("hw2", [SH, SH])
        sw1 = sb("sw1", [SH, SH // 2])
        sw2 = sb("sw2", [SH // 2, 2 * D])
        hb1 = sb("hb1", [SH, 1])
        hb2 = sb("hb2", [SH, 1])
        sb1 = sb("sb1", [SH // 2, 1])
        sb2 = sb("sb2", [P, 2 * DC])
        se_t = sb("se_t", [SE, B])
        hyp1 = sb("hyp1", [SH, B])
        hyp2 = sb("hyp2", [SH, B])
        sty1 = sb("sty1", [SH // 2, B])
        sty = sb("sty", [P, 2 * DC, B])
        soft = sb("soft", [P, 3, DC, B])
        gamma = sb("gamma", [P, B, DC])
        beta = sb("beta", [P, B, DC])
        turns_i = sb("turns_i", [P, 2, B], I32)
        turns = sb("turns", [P, 2, B])
        red = sb("red", [P, 2, B])
        co_arg = sb("co_arg", [P, 2, B])
        sn = sb("sn", [P, 2, B])
        cs = sb("cs", [P, 2, B])
        xr = sb("xr", [P, 3, PT, D])
        st = sb("st", [P, PT, 6])
        mv = sb("mv", [P, PT, 2])
        var_e = sb("var_e", [P, 2, 2 * DC])
        log_v = sb("log_v", [P, 2, 2 * DC])
        rs0 = sb("rs0", [P, 2, 2 * DC])
        sq = sb("sq", [P, 2, 2 * DC])
        rs = sb("rs", [P, 2, 2 * DC])
        st_t = sb("st_t", [P, 2 * DC, 6])
        mv_t = sb("mv_t", [P, 2 * DC, 2])
        g4 = sb("g4", [P, 2, DC])
        b4 = sb("b4", [P, 2, DC])
        gg4 = sb("gg4", [P, 2, DC])
        tmp4 = sb("tmp4", [P, 6, 2 * DC])
        co_a = sb("co_a", [P, 2, 2 * DC])
        co_b = sb("co_b", [P, 2, 2 * DC])
        rows = sb("rows", [P, GT, ROW])
        lg2 = sb("lg2", [P, GT, E])
        pick = sb("pick", [P, GT, E])
        oh1 = sb("oh1", [P, GT, E])
        oh2 = sb("oh2", [P, GT, E])
        mask = sb("mask", [P, GT, E], BF16)
        mx1 = sb("mx1", [P, GT])
        mx2 = sb("mx2", [P, GT])
        at1 = sb("at1", [P, GT])
        at2 = sb("at2", [P, GT])
        dm = sb("dm", [P, GT])
        ex = sb("ex", [P, GT])
        den = sb("den", [P, GT])
        gate1 = sb("gate1", [P, GT])
        comb = sb("comb", [P, GT, E])
        place = sb("place", [P, GT, E])
        slot_f = sb("slot_f", [P, TOPK, GT])
        slot_u = sb("slot_u", [P, TOPK, GT], U32)
        carry = sb("carry", [P, E])
        pad_at = sb("pad_at", [1, E], I32)
        cnt = sb("cnt", [1, E])
        over = sb("over", [1, E, N // ET])
        n_t = sb("n_t", [1, E])
        cum = sb("cum", [1, E, E])
        end = sb("end", [1, E])
        past = sb("past", [1, MAXT, E])
        pastn = sb("pastn", [1, MAXT, E])
        done_e = sb("done_e", [1, MAXT])
        start_t = sb("start_t", [1, MAXT])
        tf = sb("tf", [1, 8, MAXT])
        table = sb("table", [1, 6, MAXT + UNROLL], I32)
        full = sb("full", [1, len(EARLY)], I32)
        total = sb("total", [1, 1], I32)
        b1_rows = sb("b1_rows", [E * FC, P])
        b1_all = sb("b1_all", [P, E * FC])
        b2_all = sb("b2_all", [P, E * D])
        stage = sb("stage", [P, WE])
        wts = sb("wts", [P, 2 * 2 * WE], F32R)
        got = sb("got", [P, UNROLL, ETB, ROW])
        gate = sb("gate", [P, UNROLL, ETB])
        dest = sb("dest", [P, UNROLL, ETB], U32)
        b1 = sb("b1", [P, 2, FC])
        hin_hi = sb("hin_hi", [P, 2, DC * ET], F32R)
        hin_lo = sb("hin_lo", [P, 2, DC * ET], F32R)
        hid = sb("hid", [P, FC * ET])
        y_raw = sb("y_raw", [P, 2, ETB, D])
        y = sb("y", [P, 2, ETB, D])

        with ExitStack() as early:
            def sb_early(name, shape, dt=F32):
                return early.enter_context(nc.sbuf_tensor(name, shape, dt))

            xin = sb_early("xin", [P, 2, PT, D])
            z = sb_early("z", [P, 2, PT, D])
            h_t = sb_early("h_t", [P, 2, DC, PT * P])
        hid_hi = sb("hid_hi", [P, 2, FC * ET], F32R)
        hid_lo = sb("hid_lo", [P, 2, FC * ET], F32R)

        ps = ctx.enter_context(nc.psum_tensor("ps", [P, 8, NB], F32))
        zt_ps = [ps[:, 0:2, :], ps[:, 2:4, :]]
        back_ps = ps[:, 4:6, :]
        logit_ps = ps[:, 6, 0:GT * E]
        rank_ps = ps[:, 7, 0:(GT + 1) * E].rearrange("p (i e) -> p i e", e=E)
        style_ps = ps[:, 5, :]
        b1_ps = ps[:, 5, NB // 2:NB // 2 + E * FC]
        hin_ps = [ps[:, 0, :], ps[:, 1, :]]
        hid_ps = ps[:, 2:2 + HB, :]
        y_ps = [ps[:, 6, :], ps[:, 7, :]]

        angles_in = sem("angles_in")
        style_in = sem("style_in")
        small_in = sem("small_in")
        x_in = [sem("x_in0"), sem("x_in1")]
        consts = sem("consts")
        pad_ready = sem("pad_ready")
        angle = sem("angle")
        trig = sem("trig")
        style_mm = sem("style_mm")
        style_sb = sem("style_sb")
        soft_in = sem("soft_in")
        soft_ex = sem("soft_ex")
        soft_p1 = sem("soft_p1")
        soft_ln = sem("soft_ln")
        scaled = sem("scaled")
        rotated = sem("rotated")
        x_out = [sem("x_out0"), sem("x_out1"), sem("x_out2")]
        var_ready = sem("var_ready")
        log_ready = sem("log_ready")
        rs0_ready = sem("rs0_ready")
        normed = sem("normed")
        turned = sem("turned")
        coefs = sem("coefs")
        h_ready = sem("h_ready")
        logits_ready = sem("logits_ready")
        turned_back = sem("turned_back")
        rows_filled = sem("rows_filled")
        logits_read = sem("logits_read")
        dm_ready = sem("dm_ready")
        ex_ready = sem("ex_ready")
        mask_ready = sem("mask_ready")
        ranks = sem("ranks")
        slots_ready = sem("slots_ready")
        rows_sent = [sem("rows_sent0"), sem("rows_sent1")]
        full_known = sem("full_known")
        pad_idx = sem("pad_idx")
        pads_in = sem("pads_in")
        pads_fixed = sem("pads_fixed")
        table_ready = sem("table_ready")
        stage_in = sem("stage_in")
        w_high = sem("w_high")
        w_ready = sem("w_ready")
        got_in = [sem(f"got_in{i}") for i in range(UNROLL)]
        hin_t = sem("hin_t")
        hin_high = sem("hin_high")
        hin_low = sem("hin_low")
        l1_done = sem("l1_done")
        hid_read = sem("hid_read")
        hid_high = sem("hid_high")
        hid_low = sem("hid_low")
        l2_done = sem("l2_done")
        meta = sem("meta")
        y_biased = sem("y_biased")
        y_ready = sem("y_ready")
        added = sem("added")
        dve_chain = sem("dve_chain")

        block = ctx.enter_context(nc.Block())

        N_SMALL, N_STYLE = 11, 4
        N_CONSTS = 9

        counts = {}

        def load_count(eng):
            counts[eng.engine] = eng.value_load(total[:], min_val=SURE, max_val=MAXT)
            return counts[eng.engine]

        def real(eng, t):
            return counts[eng.engine] > t

        def either(eng, step, s, u):
            with eng.If(real(eng, s)):
                step(s, u, True)
            with eng.Else():
                step(s, u, False)

        def tile_loop(eng, step, unsure=either, first=0):
            for s in range(first, PEEL):
                step(s, s, True)
            load_count(eng)
            with eng.Fori(PEEL, SURE - 1, UNROLL) as s:
                for u in range(UNROLL):
                    step(s + u, PEEL + u, True)
            with eng.Fori(SURE - 1, MAXT, UNROLL) as s:
                for u in range(UNROLL):
                    unsure(eng, step, s + u, SURE - 1 + u)
            for s in range(MAXT, MAXT + STAGES - 1):
                step(s, s, False)

        def if_real(eng, t, sure):
            return nullcontext() if sure else eng.If(real(eng, t))

        def exists(s, lag):
            return not isinstance(s, int) or 0 <= s - lag < MAXT

        def tiles_of(g):
            pairs = GROUPS[g]
            return slice(pairs[0] % 2 * PT, (pairs[-1] % 2 + 1) * PT)

        def routed_at(n):
            full = [g for g in range(len(GROUPS) - 2) if GROUPS[g][-1] == n - 2]
            return full[0] + 1 if full else 0

        def later(s, tile):
            return not isinstance(s, int) or s >= tile

        @block.sync
        def _(sp):
            def load_pair(n):
                if n >= 2:
                    sp.wait_ge(rotated, n - 1)
                sp.dma_start(xin[:, n % 2], x_pairs[n]).then_inc(x_in[n % 2], 16)

            sp.dma_start(th[:, 0, :], theta.partition_broadcast(P)).then_inc(angles_in, 16)
            sp.dma_start(th[:, 1, :], phi.partition_broadcast(P)).then_inc(angles_in, 16)
            load_pair(0)
            load_pair(1)
            with nc.allow_non_contiguous_dma(reason="small per-feature columns"):
                for dst, src in (
                    (sw2[:], sty_w2),
                    (sb2[:], sty_b2.rearrange("(c p) -> p c", p=P)),
                    (g_c[:], ln_g.rearrange("(c p) -> p c", p=P)),
                    (b_c[:], ln_b.rearrange("(c p) -> p c", p=P)),
                    (rw[:], router_w.rearrange("(c p) e -> p c e", p=P)),
                    (b1_rows[:], exp_b1.rearrange("e (k p) -> (e k) p", p=P)),
                    (b2_all[:], exp_b2.rearrange("e d -> (e d)").partition_broadcast(P)),
                ):
                    sp.dma_start(dst, src).then_inc(small_in, 16)
            sp.wait_ge(pad_ready, 2)
            sp.dma_start(sent_tile(E * CAP), pad_rows[:]).then_inc(pads_fixed, 16)
            sp.dma_start(out[N:N + ET, :].rearrange("(r p) d -> p r d", p=P), pad_rows[:, :, 0:D]).then_inc(pads_fixed, 16)
            for n in range(PAIRS):
                sp.wait_ge(rotated, n + 1)
                sp.dma_start(out_pairs[n], xr[:, n % 3]).then_inc(x_out[n % 3], 16)
                if n + 2 < PAIRS:
                    load_pair(n + 2)

            def load_tile(i, row):
                sp.dma_start(got[:, i], sent_tile(row)).then_inc(got_in[i], 16)

            def is_full(j):
                return sp.value_load(full[0:1, j:j + 1], min_val=0, max_val=1)

            def load_early(left):
                sp.wait_ge(full_known, 1 if left == EARLY[0] else 2)
                for half in range(2):
                    sp.wait_ge(rows_sent[half], 16 * TOPK * PT * len(range(half, PAIRS - left, 2)))
                for j in range(len(EARLY)):
                    if EARLY[j] == left:
                        with sp.If(is_full(j) > 0):
                            load_tile(j, j * ET)

            load_early(2)
            sp.wait_ge(pad_idx, 1)
            for e in range(E):
                if e == E // 2:
                    load_early(1)
                row = sp.value_load(pad_at[0:1, e:e + 1], min_val=e * CAP, max_val=e * CAP + N)
                sp.dma_start(sent_tile(row), pad_rows[:]).then_inc(pads_in, 16)

            sp.wait_ge(pads_in, 16 * E)
            sp.wait_ge(pads_fixed, 32)
            for half in range(2):
                sp.wait_ge(rows_sent[half], 16 * TOPK * PT * (PAIRS // 2))
            with sp.If(is_full(0) < 1):
                load_tile(0, 0)
            sp.wait_ge(table_ready, 1)
            for j in range(1, len(EARLY)):
                with sp.If(is_full(j) < 1):
                    load_tile(j, sp.value_load(table[0:1, T_BASE, j:j + 1], min_val=0, max_val=E * CAP))

            def step(s, u, sure):
                if not exists(s, 0) or not later(s, len(EARLY)) or not sure:
                    return
                i = u % UNROLL
                if later(s, UNROLL):
                    sp.wait_ge(hin_t, s - (UNROLL - 1))
                    sp.wait_ge(meta, s - (UNROLL - 1))
                load_tile(i, sp.value_load(table[0:1, T_BASE, bass.ds(s, 1)], min_val=0, max_val=E * CAP))

            def load_if_real(sp, step, s, u):
                with sp.If(real(sp, s)):
                    step(s, u, True)

            tile_loop(sp, step, load_if_real)

        @block.gpsimd
        def _(pool):
            def load_expert(e):
                pool.dma_start(stage[:, 0:DC * FF].rearrange("p (c f) -> p c f", c=DC),
                               exp_w1[e].rearrange("(c p) f -> p c f", p=P)).then_inc(stage_in, 16)
                pool.dma_start(stage[:, DC * FF:WE].rearrange("p (c d) -> p c d", c=FC),
                               exp_w2[e].rearrange("(c p) d -> p c d", p=P)).then_inc(stage_in, 16)

            for dst, src in (
                (hw2[:], hyp_w2),
                (hb2[:], hyp_b2.rearrange("(p a) -> p a", a=1)),
                (sw1[:], sty_w1),
                (sb1[:], sty_b1.rearrange("(p a) -> p a", a=1)),
            ):
                pool.dma_start(dst, src).then_inc(style_in, 16)
            nc.gpsimd.memset(ident[:], 1.0)
            nc.gpsimd.memset(before[:], 1.0)
            nc.gpsimd.memset(upto[:], 1.0)
            nc.gpsimd.memset(ones[:], 1.0)
            nc.gpsimd.memset(pad_rows[:], 0.0).then_inc(consts, 1)
            pool.wait_ge(consts, 1)
            nc.gpsimd.affine_select(out=ident[:], in_=ident[:], compare_op=ALU.is_equal, fill=0.0, base=0,
                                    pattern=[[-1, P]], channel_multiplier=1).then_inc(consts, 1)
            nc.gpsimd.affine_select(out=before[:], in_=before[:], compare_op=ALU.is_gt, fill=0.0, base=0,
                                    pattern=[[1, P]], channel_multiplier=-1).then_inc(consts, 1)
            nc.gpsimd.iota(iota_p[:], pattern=[[0, 1]], base=0, channel_multiplier=1,
                           allow_small_or_imprecise_dtypes=True).then_inc(consts, 1)
            nc.gpsimd.iota(pad_rows[:, :, D + E], pattern=[[P, ETB]], base=N, channel_multiplier=1,
                           allow_small_or_imprecise_dtypes=True).then_inc(pad_ready, 2)
            nc.gpsimd.affine_select(out=upto[:], in_=upto[:], compare_op=ALU.is_ge, fill=0.0, base=0,
                                    pattern=[[1, E], [-1, E]], channel_multiplier=0).then_inc(consts, 1)
            nc.gpsimd.iota(rev[:], pattern=[[-1, E]], base=E, channel_multiplier=0,
                           allow_small_or_imprecise_dtypes=True).then_inc(consts, 1)
            nc.gpsimd.iota(ebase[:], pattern=[[CAP, E]], base=0, channel_multiplier=0,
                           allow_small_or_imprecise_dtypes=True)
            nc.gpsimd.iota(carry[:], pattern=[[CAP, E]], base=0, channel_multiplier=0,
                           allow_small_or_imprecise_dtypes=True).then_inc(consts, 1)
            nc.gpsimd.iota(tok[:], pattern=[[P, GT]], base=0, channel_multiplier=1,
                           allow_small_or_imprecise_dtypes=True).then_inc(consts, 1)
            nc.gpsimd.iota(tiles[:], pattern=[[1, MAXT]], base=0, channel_multiplier=0,
                           allow_small_or_imprecise_dtypes=True)
            nc.gpsimd.iota(thresholds[:], pattern=[[ET, N // ET]], base=0, channel_multiplier=0,
                           allow_small_or_imprecise_dtypes=True).then_inc(consts, 1)
            pool.wait_ge(x_in[1], 16)
            load_expert(0)
            pool.wait_ge(w_high, 1)
            nc.gpsimd.tensor_tensor(wts[:, WE:2 * WE], stage[:], wts[:, 0:WE], ALU.subtract).then_inc(w_ready, 1)
            pool.wait_ge(w_ready, 1)
            load_expert(1)

            def split_expert_1():
                pool.wait_ge(w_high, 2)
                nc.gpsimd.tensor_tensor(wts[:, 3 * WE:4 * WE], stage[:], wts[:, 2 * WE:3 * WE],
                                        ALU.subtract).then_inc(w_ready, 1)
                pool.wait_ge(w_ready, 2)
                load_expert(2)

            for g, pairs in enumerate(GROUPS):
                pool.wait_ge(slots_ready, g + 1)
                for n in pairs:
                    pool.wait_ge(rows_filled, n + 1)
                    for i in range(n % 2 * PT, (n % 2 + 1) * PT):
                        for k in range(TOPK):
                            nc.gpsimd.indirect_dma_start(
                                out=sent, out_offset=bass.IndirectOffsetOnAxis(ap=slot_u[:, k, i:i + 1], axis=0),
                                in_=rows[:, i, :], in_offset=None).then_inc(rows_sent[n % 2], 16)

            split_expert_1()

            for i in range(3):
                pool.wait_ge(x_out[i], 16 * len(range(i, PAIRS, 3)))
            pool.wait_ge(pads_fixed, 32)
            pool.wait_ge(table_ready, 1)

            def step(s, u, sure):
                if not exists(s, STAGES - 1):
                    return
                t = s - (STAGES - 1)
                i = (u - (STAGES - 1)) % UNROLL
                with if_real(pool, t, sure):
                    pool.wait_ge(pads_fixed, 32)
                    if later(s, STAGES):
                        pool.wait_ge(added, 16 * ETB * t if isinstance(s, int) else adds)
                    pool.wait_ge(y_ready, t + 1 if isinstance(s, int) else outputs)
                    for r in range(ETB):
                        nc.gpsimd.indirect_dma_start(
                            out=out, out_offset=bass.IndirectOffsetOnAxis(ap=dest[:, i, r:r + 1], axis=0),
                            in_=y[:, i % 2, r, :], in_offset=None, compute_op=ALU.add).then_inc(added, 16)
                    if not isinstance(s, int):
                        pool.reg_add(outputs, outputs, 1)
                        pool.reg_add(adds, adds, 16 * ETB)
                    split = pool.value_load(table[0:1, T_SPLIT, bass.ds(t, 1)], min_val=0, max_val=1)
                    with pool.If(split > 0):
                        e = pool.value_load(table[0:1, T_EXPERT, bass.ds(t, 1)], min_val=0, max_val=E - 1)
                        slot = pool.value_load(table[0:1, T_SLOT, bass.ds(t, 1)], min_val=0, max_val=1)
                        more = pool.value_load(table[0:1, T_LOAD, bass.ds(t, 1)], min_val=0, max_val=E - 1)
                        pool.wait_ge(w_high, e + 3)
                        nc.gpsimd.tensor_tensor(wts[:, bass.ds(slot * (2 * WE) + WE, WE)], stage[:],
                                                wts[:, bass.ds(slot * (2 * WE), WE)],
                                                ALU.subtract).then_inc(w_ready, 1)
                        with pool.If(more > 0):
                            pool.wait_ge(w_ready, e + 3)
                            load_expert(more)

            outputs, adds = pool.alloc_register("outputs"), pool.alloc_register("adds")
            pool.reg_mov(outputs, PEEL - (STAGES - 1) + 1)
            pool.reg_mov(adds, 16 * ETB * (PEEL - (STAGES - 1)))
            tile_loop(pool, step, lambda pool, step, s, u: step(s, u, False))
            pool.wait_ge(added, counts[pool.engine] * (16 * ETB))

        @block.scalar
        def _(act):
            nc.scalar.preload_act_table_set("trig_and_small")
            for dst, src in (
                (ids_i[:], itok.partition_broadcast(SUBJ)),
                (emb[:], subj_emb),
                (hw1[:], hyp_w1),
                (hb1[:], hyp_b1.rearrange("(p a) -> p a", a=1)),
            ):
                act.dma_start(dst, src).then_inc(small_in, 16)
            act.wait_ge(angle, 1)
            nc.scalar.activation(sn[:], red[:], ACT.Sin).then_inc(trig, 1)
            nc.scalar.activation(cs[:], co_arg[:], ACT.Sin).then_inc(trig, 1)
            act.wait_ge(trig, 2)

            def products(n, j):
                if j == 0:
                    act.wait_ge(x_in[n % 2], 16 * (n // 2 + 1))
                    if n >= 2:
                        act.wait_ge(turned, n - 1)
                    if n >= 3:
                        act.wait_ge(x_out[n % 3], 16 * (n // 3))
                        act.wait_ge(normed, n - 2)
                b = 2 * n + j
                src, dst, side = (v[:, 2 * j:2 * j + 2, :].rearrange("p i (g a r) -> p (i g) a r", a=2, r=2)
                                  for v in (xin[:, n % 2], xr[:, n % 3], z[:, n % 2]))
                for a in range(2):
                    nc.scalar.mul(dst[:, :, a, :], src[:, :, a, :], cs[:, a, b:b + 1])
                    last = nc.scalar.mul(side[:, :, a, :], src[:, :, a, :], sn[:, a, b:b + 1])
                last.then_inc(scaled, 1)

            def apply_norm(n):
                act.wait_ge(coefs, n + 1)
                if n >= 2:
                    act.wait_ge(turned_back, n - 1)
                for j in range(2):
                    for c in range(DC):
                        k = j * DC + c
                        last = nc.scalar.activation(h_t[:, n % 2, c, j * S:(j + 1) * S],
                                                    zt_ps[n % 2][:, j, c * S:(c + 1) * S], ACT.Identity,
                                                    bias=co_b[:, n % 2, k:k + 1], scale=co_a[:, n % 2, k:k + 1])
                last.then_inc(h_ready, 1)

            def fill_rows(n):
                act.wait_ge(turned_back, n + 1)
                if n >= 2:
                    act.wait_ge(rows_sent[n % 2], 16 * TOPK * PT * (n // 2))
                nc.scalar.copy(rows[:, (n % 2) * PT:(n % 2 + 1) * PT, 0:D],
                               back_ps.rearrange("p j (i d) -> p (j i) d", d=D)).then_inc(rows_filled, 1)

            def gate_exp(g):
                act.wait_ge(dm_ready, g + 1)
                nc.scalar.activation(ex[:, tiles_of(g)], dm[:, tiles_of(g)], ACT.Exp).then_inc(ex_ready, 1)

            def inverse_roots(n):
                act.wait_ge(var_ready, n + 1)
                nc.scalar.activation(log_v[:], var_e[:], ACT.Ln).then_inc(log_ready, 1)
                act.wait_ge(log_ready, n + 1)
                nc.scalar.activation(rs0[:], log_v[:], ACT.Exp, scale=-0.5).then_inc(rs0_ready, 1)

            products(0, 0)
            products(0, 1)
            nc.scalar.preload_act_table_set("natural_log_exp_and_others")
            products(1, 0)
            inverse_roots(0)
            products(1, 1)
            act.wait_ge(stage_in, 32)
            nc.scalar.copy(wts[:, 0:WE], stage[:]).then_inc(w_high, 1)
            inverse_roots(1)
            products(2, 0)
            products(2, 1)
            act.wait_ge(soft_in, 1)
            nc.scalar.activation(soft[:, 1], soft[:, 0], ACT.Exp, scale=-1.0).then_inc(soft_ex, 1)
            act.wait_ge(soft_p1, 1)
            nc.scalar.activation(soft[:, 2], soft[:, 1], ACT.Ln).then_inc(soft_ln, 1)
            apply_norm(0)
            for n in range(2, PAIRS + 1):
                if n + 1 < PAIRS:
                    products(n + 1, 0)
                inverse_roots(n)
                if n + 1 < PAIRS:
                    products(n + 1, 1)
                if routed_at(n):
                    fill_rows(n - 2)
                    gate_exp(routed_at(n) - 1)
                    apply_norm(n - 1)
                else:
                    apply_norm(n - 1)
                    if n == PAIRS:
                        gate_exp(len(GROUPS) - 2)
                    fill_rows(n - 2)
            fill_rows(PAIRS - 1)
            gate_exp(len(GROUPS) - 1)
            act.wait_ge(stage_in, 64)
            nc.scalar.copy(wts[:, 2 * WE:3 * WE], stage[:]).then_inc(w_high, 1)

            def step(s, u, sure):
                if exists(s, 0) and sure:
                    i = u % 2
                    act.wait_ge(hin_t, s + 1)
                    if later(s, 2):
                        act.wait_ge(l1_done, (s - 1) * HB)
                    nc.scalar.copy(hin_hi[:, i, :], hin_ps[i]).then_inc(hin_high, 1)
                if exists(s, 1):
                    with if_real(act, s - 1, sure):
                        t, i = s - 1, (u - 1) % 2
                        act.wait_ge(meta, t + 1)
                        for k in range(FC):
                            if later(s, 2) and k % (FC // 2) == 0:
                                act.wait_ge(hid_low, (t - 1) * 2 + (k // (FC // 2) + 1))
                            if k % 2 == 0:
                                act.wait_ge(l1_done, t * HB + (k // 2 + 1))
                            last = nc.scalar.activation(hid[:, k * ET:(k + 1) * ET],
                                                        hid_ps[:, k // 2, (k % 2) * ET:(k % 2 + 1) * ET], ACT.Relu,
                                                        bias=b1[:, i, k:k + 1])
                            if k % 2 == 1:
                                last.then_inc(hid_read, 1)
                if exists(s, 2):
                    with if_real(act, s - 2, sure):
                        t, i = s - 2, (u - 2) % UNROLL
                        act.wait_ge(y_biased, t + 1)
                        if later(s, 4):
                            act.wait_ge(added, (t - 1) * (16 * ETB))
                        for r in range(ETB):
                            last = nc.scalar.mul(y[:, i % 2, r, :], y_raw[:, i % 2, r, :], gate[:, i, r:r + 1])
                        last.then_inc(y_ready, 1)
                        if isinstance(t, int) and t == 0:
                            act.wait_ge(table_ready, 1)
                        split = act.value_load(table[0:1, T_SPLIT, bass.ds(t, 1)], min_val=0, max_val=1)
                        with act.If(split > 0):
                            e = act.value_load(table[0:1, T_EXPERT, bass.ds(t, 1)], min_val=0, max_val=E - 1)
                            slot = act.value_load(table[0:1, T_SLOT, bass.ds(t, 1)], min_val=0, max_val=1)
                            act.wait_ge(stage_in, (e + 3) * 32)
                            nc.scalar.copy(wts[:, bass.ds(slot * (2 * WE), WE)], stage[:]).then_inc(w_high, 1)

            tile_loop(act, step)

        @block.vector
        def _(dve):
            links = [0]

            def link(ins):
                links[0] += 1
                ins.then_inc(dve_chain, 1)
                dve.wait_ge(dve_chain, links[0])

            link(nc.vector.memset(var_e[:], 1.0))
            dve.wait_ge(angles_in, 32)
            link(nc.vector.tensor_scalar(turns_i[:], th[:], 1.0 / (TWO_PI_A + TWO_PI_B), None, ALU.mult))
            link(nc.vector.tensor_copy(turns[:], turns_i[:]))
            link(nc.vector.scalar_tensor_tensor(red[:], turns[:], -TWO_PI_A, th[:], ALU.mult, ALU.add))
            link(nc.vector.scalar_tensor_tensor(red[:], turns[:], -TWO_PI_B, red[:], ALU.mult, ALU.add))
            link(nc.vector.scalar_tensor_tensor(co_arg[:], red[:], -1.0, red[:], ALU.mult, ALU.max))
            nc.vector.tensor_scalar(co_arg[:], co_arg[:], -1.0, HALF_PI, ALU.mult, ALU.add).then_inc(angle, 1)

            def style_start():
                dve.wait_ge(small_in, 16 * N_SMALL)
                dve.wait_ge(style_in, 16 * N_STYLE)
                dve.wait_ge(consts, N_CONSTS)
                link(nc.vector.tensor_copy(ids[:], ids_i[:]))
                nc.vector.tensor_scalar(onehot[:], ids[:], iota_p[0:SUBJ, :], None, ALU.is_equal).then_inc(style_sb, 1)
                for j in range(2):
                    nc.vector.tensor_copy(g4[:, j, :], g_c[:])
                    last = nc.vector.tensor_copy(b4[:, j, :], b_c[:])
                link(last)
                nc.vector.tensor_tensor(gg4[:], g4[:], g4[:], ALU.mult)

            def style_embedding():
                dve.wait_ge(style_mm, 1)
                nc.vector.tensor_copy(se_t[:], style_ps[0:SE, 0:B]).then_inc(style_sb, 1)

            def style_hyper1():
                dve.wait_ge(style_mm, 2)
                nc.vector.tensor_scalar(hyp1[:], style_ps[:, B:2 * B], hb1[:], 0.0, ALU.add, ALU.max).then_inc(style_sb, 1)

            def style_hyper2():
                dve.wait_ge(style_mm, 3)
                nc.vector.tensor_scalar(hyp2[:], style_ps[:, 2 * B:3 * B], hb2[:], None, ALU.add).then_inc(style_sb, 1)

            def style_hidden():
                dve.wait_ge(style_mm, 4)
                nc.vector.tensor_scalar(sty1[:], style_ps[0:SH // 2, 3 * B:4 * B], sb1[:], 0.0, ALU.add,
                                        ALU.max).then_inc(style_sb, 1)

            def style_out():
                dve.wait_ge(style_mm, 5)
                link(nc.vector.tensor_tensor(sty[:], style_ps[:, 4 * B:8 * B].rearrange("p (c b) -> p c b", b=B),
                                             sb2[:, :, None].to_broadcast([P, 2 * DC, B]), ALU.add))
                nc.vector.tensor_copy(b1_all[:], b1_ps)
                nc.vector.tensor_copy(beta[:].rearrange("p b c -> p c b"), sty[:, DC:, :])
                nc.vector.scalar_tensor_tensor(soft[:, 0], sty[:, 0:DC, :], -1.0, sty[:, 0:DC, :], ALU.mult,
                                               ALU.max).then_inc(soft_in, 1)

            def style_softplus():
                dve.wait_ge(soft_ex, 1)
                nc.vector.tensor_scalar(soft[:, 1], soft[:, 1], 1.0, None, ALU.add).then_inc(soft_p1, 1)
                dve.wait_ge(soft_ln, 1)
                link(nc.vector.scalar_tensor_tensor(soft[:, 2], sty[:, 0:DC, :], 0.0, soft[:, 2], ALU.max, ALU.add))
                link(nc.vector.tensor_scalar(gamma[:].rearrange("p b c -> p c b"), soft[:, 2], SOFTPLUS_EPS, None,
                                             ALU.add))

            def rotate(n):
                xo, side = (v.rearrange("p i (g r) -> p (i g) r", r=2) for v in (xr[:, n % 3], z[:, n % 2]))
                dve.wait_ge(scaled, 2 * (n + 1))
                nc.vector.tensor_tensor(xo[:, :, 0], xo[:, :, 0], side[:, :, 1], ALU.add)
                nc.vector.tensor_tensor(xo[:, :, 1], xo[:, :, 1], side[:, :, 0], ALU.subtract).then_inc(rotated, 1)
                dve.wait_ge(rotated, n + 1)

            def token_stats(n):
                for i in range(PT):
                    last = nc.vector.bn_stats(st[:, i, :], xr[:, n % 3, i, :])
                return last

            def time_stats(n):
                dve.wait_ge(turned, n + 1)
                for j in range(2):
                    for c in range(DC):
                        last = nc.vector.bn_stats(st_t[:, j * DC + c, :], zt_ps[n % 2][:, j, c * S:(c + 1) * S])
                return last

            def token_moments():
                for i in range(PT):
                    last = nc.vector.bn_aggr(mv[:, i, :], st[:, i, :])
                return last

            def time_moments():
                for k in range(2 * DC):
                    last = nc.vector.bn_aggr(mv_t[:, k, :], st_t[:, k, :])
                return last

            g_f, b_f, gg_f = (v[:].rearrange("p j c -> p (j c)") for v in (g4, b4, gg4))

            def token_variances():
                return nc.vector.tensor_scalar(var_e[:, 0, :], mv[:, :, 1], LN_EPS, None, ALU.add)

            def time_variances():
                mean = tmp4[:, 0, :]
                nc.vector.tensor_tensor(tmp4[:, 1, :], mv_t[:, :, 1], gg_f, ALU.mult)
                link(nc.vector.tensor_tensor(mean, mv_t[:, :, 0], g_f, ALU.mult))
                nc.vector.tensor_scalar(var_e[:, 1, :], tmp4[:, 1, :], IN_EPS, None, ALU.add).then_inc(var_ready, 1)
                link(nc.vector.tensor_tensor(mean, mean, b_f, ALU.add))
                nc.vector.tensor_tensor(tmp4[:, 2, :], b_f, mean, ALU.subtract)

            def newton(n):
                dve.wait_ge(rs0_ready, n + 1)
                link(nc.vector.tensor_tensor(sq[:], rs0[:], rs0[:], ALU.mult))
                link(nc.vector.scalar_tensor_tensor(sq[:], sq[:], -0.5, var_e[:], ALU.mult, ALU.mult))
                link(nc.vector.scalar_tensor_tensor(rs[:], sq[:], 1.5, rs0[:], ALU.add, ALU.mult))

            def normalise(n, i):
                return nc.vector.tensor_scalar(z[:, n % 2, i, :], xr[:, n % 3, i, :], mv[:, i, 0:1], rs[:, 0, i:i + 1],
                                               ALU.subtract, ALU.mult)

            def normalise_all(n):
                for i in range(PT):
                    last = normalise(n, i)
                last.then_inc(normed, 1)

            def time_scale(n):
                ga = gamma[:, 2 * n:2 * n + 2, :].rearrange("p b c -> p (b c)")
                return nc.vector.tensor_tensor(tmp4[:, 3, :], rs[:, 1, :], ga, ALU.mult)

            def time_a(n):
                nc.vector.tensor_tensor(co_a[:, n % 2, :], tmp4[:, 3, :], g_f, ALU.mult)
                return nc.vector.tensor_tensor(tmp4[:, 4, :], tmp4[:, 2, :], tmp4[:, 3, :], ALU.mult)

            def time_b(n):
                be = beta[:, 2 * n:2 * n + 2, :].rearrange("p b c -> p (b c)")
                nc.vector.tensor_tensor(co_b[:, n % 2, :], tmp4[:, 4, :], be, ALU.add).then_inc(coefs, 1)

            def time_coefs(n):
                link(time_scale(n))
                link(time_a(n))
                time_b(n)

            def coefs_and_normalise(n):
                time_scale(n - 1)
                link(normalise(n, 0))
                time_a(n - 1)
                link(normalise(n, 1))
                time_b(n - 1)
                normalise(n, 2)
                normalise(n, 3).then_inc(normed, 1)

            def best(src, mx, at, oh, tt):
                shape = [P, tt.stop - tt.start, E]
                experts = rev[:, None, :].to_broadcast(shape)
                link(nc.vector.tensor_reduce(mx[:, tt], src, AX_X, ALU.max))
                link(nc.vector.tensor_tensor(pick[:, tt], src, mx[:, tt, None].to_broadcast(shape), ALU.is_equal))
                link(nc.vector.tensor_tensor(pick[:, tt], pick[:, tt], experts, ALU.mult))
                link(nc.vector.tensor_reduce(at[:, tt], pick[:, tt], AX_X, ALU.max))
                link(nc.vector.tensor_tensor(oh[:, tt], experts, at[:, tt, None].to_broadcast(shape), ALU.is_equal))

            def early_full(left):
                jj = slice(EARLY.index(left), EARLY.index(left) + EARLY.count(left))
                nc.vector.tensor_scalar(full[:, jj], thresholds[:, jj.start + 1:jj.stop + 1], carry[0:1, 0:1], None,
                                        ALU.is_le).then_inc(full_known, 1)

            def route(g):
                pairs, tt = GROUPS[g], tiles_of(g)
                count = tt.stop - tt.start
                shape = [P, count, E]
                lg = logit_ps[:, tt.start * E:tt.stop * E].rearrange("p (i e) -> p i e", e=E)
                dve.wait_ge(logits_ready, pairs[-1] + 1)
                best(lg, mx1, at1, oh1, tt)
                nc.vector.scalar_tensor_tensor(lg2[:, tt], oh1[:, tt], FAR, lg, ALU.mult, ALU.add).then_inc(logits_read, 1)
                dve.wait_ge(logits_read, g + 1)
                best(lg2[:, tt], mx2, at2, oh2, tt)
                nc.vector.tensor_tensor(dm[:, tt], mx2[:, tt], mx1[:, tt], ALU.subtract).then_inc(dm_ready, 1)
                if g >= 1:
                    dve.wait_ge(ranks, g)
                nc.vector.tensor_tensor(mask[:, tt], oh1[:, tt], oh2[:, tt], ALU.add).then_inc(mask_ready, 1)
                for n in pairs:
                    if n >= 2:
                        dve.wait_ge(rows_sent[n % 2], 16 * TOPK * PT * (n // 2))
                nc.vector.tensor_copy(rows[:, tt, D + E], tok[:, tt])
                dve.wait_ge(ex_ready, g + 1)
                nc.vector.tensor_scalar(den[:, tt], ex[:, tt], 1.0, None, ALU.add)
                nc.vector.tensor_tensor(comb[:, tt], oh2[:, tt], ex[:, tt, None].to_broadcast(shape), ALU.mult)
                dve.wait_ge(ranks, g + 1)
                link(nc.vector.tensor_tensor(place[:, tt], rank_ps[:, 0:count, :],
                                             carry[:, None, :].to_broadcast(shape), ALU.add))
                nc.vector.reciprocal(gate1[:, tt], den[:, tt])
                nc.vector.tensor_tensor(comb[:, tt], comb[:, tt], oh1[:, tt], ALU.add)
                nc.vector.tensor_tensor(pick[:, tt], place[:, tt], oh1[:, tt], ALU.mult)
                link(nc.vector.tensor_tensor(lg2[:, tt], place[:, tt], oh2[:, tt], ALU.mult))
                nc.vector.tensor_tensor(rows[:, tt, D:D + E], comb[:, tt], gate1[:, tt, None].to_broadcast(shape), ALU.mult)
                nc.vector.tensor_reduce(slot_f[:, 0, tt], pick[:, tt], AX_X, ALU.add)
                nc.vector.tensor_reduce(slot_f[:, 1, tt], lg2[:, tt], AX_X, ALU.add)
                link(nc.vector.tensor_tensor(carry[:], carry[:], rank_ps[:, count, :], ALU.add))
                if pairs[-1] % 2 == 1:
                    nc.vector.tensor_scalar(tok[:], tok[:], float(GT * P), None, ALU.add)
                nc.vector.tensor_copy(slot_u[:, :, tt], slot_f[:, :, tt]).then_inc(slots_ready, 1)

            rotate(0)
            link(token_stats(0))
            link(token_moments())
            token_variances().then_inc(var_ready, 1)
            style_start()
            newton(0)
            normalise_all(0)
            style_embedding()
            rotate(1)
            style_hyper1()
            token_stats(1)
            style_hyper2()
            link(time_stats(0))
            token_moments()
            link(time_moments())
            token_variances()
            time_variances()
            style_hidden()
            newton(1)
            normalise_all(1)
            style_out()
            rotate(2)
            style_softplus()
            time_coefs(0)
            for n in range(2, PAIRS):
                if n > 2:
                    rotate(n)
                token_stats(n)
                link(time_stats(n - 1))
                token_moments()
                link(time_moments())
                token_variances()
                time_variances()
                if routed_at(n):
                    route(routed_at(n) - 1)
                if routed_at(n) == len(GROUPS) - 2:
                    early_full(2)
                newton(n)
                coefs_and_normalise(n)
            link(time_stats(PAIRS - 1))
            link(time_moments())
            time_variances()
            newton(PAIRS)
            time_coefs(PAIRS - 1)
            route(len(GROUPS) - 2)
            early_full(1)
            route(len(GROUPS) - 1)

            dve.wait_ge(slots_ready, len(GROUPS))
            nc.vector.tensor_copy(pad_at[:], carry[0:1, :]).then_inc(pad_idx, 1)
            link(nc.vector.tensor_scalar(thresholds[:, 0:1], thresholds[:, 0:1], -1.0, None, ALU.add))
            half = FC * ET // 2

            def step(s, u, sure):
                if exists(s, 0) and sure:
                    i = u % 2
                    dve.wait_ge(hin_high, s + 1)
                    nc.vector.tensor_tensor(hin_lo[:, i, :], hin_ps[i], hin_hi[:, i, :], ALU.subtract).then_inc(hin_low, 1)
                if exists(s, 1):
                    with if_real(dve, s - 1, sure):
                        t, i, k = s - 1, (u - 1) % 2, (u - 1) % UNROLL
                        e = dve.value_load(table[0:1, T_EXPERT, bass.ds(t, 1)], min_val=0, max_val=E - 1)
                        dve.wait_ge(hin_t, t + 1)
                        if later(s, 1 + UNROLL):
                            dve.wait_ge(added, (t - (UNROLL - 1)) * (16 * ETB))
                        nc.vector.tensor_copy(b1[:, i, :], b1_all[:, bass.ds(e * FC, FC)])
                        nc.vector.tensor_copy(gate[:, k, :], got[:, k, :, bass.ds(e + D, 1)])
                        nc.vector.tensor_copy(dest[:, k, :], got[:, k, :, D + E]).then_inc(meta, 1)
                        if later(s, 3):
                            dve.wait_ge(l2_done, t - 1)
                        for h in range(2):
                            cols = slice(h * half, (h + 1) * half)
                            dve.wait_ge(hid_read, t * HB + (h + 1) * (HB // 2))
                            nc.vector.tensor_copy(hid_hi[:, i, cols], hid[:, cols]).then_inc(hid_high, 1)
                            dve.wait_ge(hid_high, t * 2 + (h + 1))
                            nc.vector.tensor_tensor(hid_lo[:, i, cols], hid[:, cols], hid_hi[:, i, cols],
                                                    ALU.subtract).then_inc(hid_low, 1)
                if exists(s, 2):
                    with if_real(dve, s - 2, sure):
                        t, i = s - 2, (u - 2) % 2
                        e = dve.value_load(table[0:1, T_EXPERT, bass.ds(t, 1)], min_val=0, max_val=E - 1)
                        dve.wait_ge(l2_done, t + 1)
                        if later(s, 4):
                            dve.wait_ge(y_ready, t - 1)
                        nc.vector.tensor_tensor(y_raw[:, i], y_ps[i].rearrange("p (r d) -> p r d", d=D),
                                                b2_all[:, None, bass.ds(e * D, D)].to_broadcast([P, ETB, D]),
                                                ALU.add).then_inc(y_biased, 1)

            step(0, 0, True)
            link(nc.vector.tensor_tensor(cnt[:], carry[0:1, :], ebase[0:1, :], ALU.subtract))
            link(nc.vector.tensor_tensor(over[:], cnt[:, :, None].to_broadcast([1, E, N // ET]),
                                         thresholds[:, None, :].to_broadcast([1, E, N // ET]), ALU.is_gt))
            link(nc.vector.tensor_reduce(n_t[:], over[:], AX_X, ALU.add))
            link(nc.vector.tensor_tensor(cum[:], upto[:], n_t[:, None, :].to_broadcast([1, E, E]), ALU.mult))
            link(nc.vector.tensor_reduce(end[:], cum[:], AX_X, ALU.add))
            link(nc.vector.tensor_tensor(past[:], tiles[:, :, None].to_broadcast([1, MAXT, E]),
                                         end[:, None, :].to_broadcast([1, MAXT, E]), ALU.is_ge))
            link(nc.vector.tensor_tensor(pastn[:], past[:], n_t[:, None, :].to_broadcast([1, MAXT, E]), ALU.mult))
            nc.vector.tensor_reduce(done_e[:], past[:], AX_X, ALU.add)
            link(nc.vector.tensor_reduce(start_t[:], pastn[:], AX_X, ALU.add))
            f = [tf[:, k, :] for k in range(8)]
            nc.vector.tensor_scalar(f[T_EXPERT], done_e[:], float(E - 1), None, ALU.min)
            nc.vector.tensor_tensor(f[6], tiles[:], start_t[:], ALU.subtract)
            nc.vector.tensor_scalar(f[T_BASE], done_e[:], float(CAP), None, ALU.mult)
            nc.vector.tensor_copy(total[:], end[:, E - 1:E])
            nc.vector.memset(f[T_SPLIT], 0.0)
            link(nc.vector.tensor_scalar(f[7], done_e[:], float(E - 2), None, ALU.is_lt))
            link(nc.vector.tensor_tensor(tf[:, T_SPLIT, 0:MAXT - 1], done_e[:, 1:], done_e[:, 0:MAXT - 1],
                                         ALU.subtract))
            nc.vector.tensor_scalar(f[T_NEED], f[T_EXPERT], 1.0, None, ALU.add)
            nc.vector.tensor_copy(f[T_SLOT], f[T_EXPERT])
            nc.vector.scalar_tensor_tensor(f[T_BASE], f[6], float(ET), f[T_BASE], ALU.mult, ALU.add)
            nc.vector.tensor_scalar(f[T_LOAD], done_e[:], 3.0, None, ALU.add)
            link(nc.vector.tensor_tensor(f[T_SPLIT], f[T_SPLIT], f[7], ALU.mult))
            nc.vector.tensor_scalar(f[T_BASE], f[T_BASE], float(E * CAP), None, ALU.min)
            link(nc.vector.tensor_scalar(f[7], done_e[:], float(E - 3), None, ALU.is_lt))
            link(nc.vector.tensor_tensor(f[T_LOAD], f[T_LOAD], f[7], ALU.mult))
            link(nc.vector.tensor_copy(table[:, :, 0:MAXT], tf[:, 0:6, :]))
            nc.vector.tensor_scalar(table[:, T_SLOT, 0:MAXT], table[:, T_SLOT, 0:MAXT], 1, None,
                                    ALU.bitwise_and).then_inc(table_ready, 1)
            dve.wait_ge(table_ready, 1)
            tile_loop(dve, step, first=1)

        @block.tensor
        def _(pe):
            pe.wait_ge(small_in, 16 * N_SMALL)
            pe.wait_ge(style_in, 16 * N_STYLE)
            pe.wait_ge(consts, N_CONSTS)
            pe.wait_ge(style_sb, 1)
            nc.tensor.matmul(style_ps[0:SE, 0:B], emb[:], onehot[:], start=True, stop=True).then_inc(style_mm, 1)

            def style_rest():
                pe.wait_ge(style_sb, 2)
                nc.tensor.matmul(style_ps[:, B:2 * B], hw1[:], se_t[:], start=True, stop=True).then_inc(style_mm, 1)
                pe.wait_ge(style_sb, 3)
                nc.tensor.matmul(style_ps[:, 2 * B:3 * B], hw2[:], hyp1[:], start=True, stop=True).then_inc(style_mm, 1)
                pe.wait_ge(style_sb, 4)
                nc.tensor.transpose(b1_ps, b1_rows[:], ident[0:E * FC, 0:E * FC])
                nc.tensor.matmul(style_ps[0:SH // 2, 3 * B:4 * B], sw1[:], hyp2[:], start=True,
                                 stop=True).then_inc(style_mm, 1)
                pe.wait_ge(style_sb, 5)
                for c in range(2 * DC):
                    last = nc.tensor.matmul(style_ps[:, (4 + c) * B:(5 + c) * B], sw2[:, c * P:(c + 1) * P], sty1[:],
                                            start=True, stop=True)
                last.then_inc(style_mm, 1)

            def turn(n):
                pe.wait_ge(normed, n + 1)
                if n >= 2:
                    pe.wait_ge(h_ready, n - 1)
                for i in range(PT):
                    for c in range(DC):
                        q = c * S + (i % 2) * P
                        last = nc.tensor.transpose(zt_ps[n % 2][:, i // 2, q:q + P], z[:, n % 2, i, c * P:(c + 1) * P],
                                                   ident[:])
                last.then_inc(turned, 1)

            def logits_and_back(n):
                pe.wait_ge(h_ready, n + 1)
                if n == 0:
                    pe.wait_ge(soft_in, 1)
                read = len([g for g in range(len(GROUPS)) if GROUPS[g][-1] < n])
                if read:
                    pe.wait_ge(logits_read, read)
                for i in range(PT):
                    k = (n % 2) * PT + i
                    for c in range(DC):
                        last = nc.tensor.matmul(logit_ps[:, k * E:(k + 1) * E], h_t[:, n % 2, c, i * P:(i + 1) * P],
                                         rw[:, c, :], start=(c == 0), stop=(c == DC - 1))
                last.then_inc(logits_ready, 1)
                if n >= 1:
                    pe.wait_ge(rows_filled, n)
                for i in range(PT):
                    for c in range(DC):
                        q = (i % 2) * D + c * P
                        last = nc.tensor.transpose(back_ps[:, i // 2, q:q + P], h_t[:, n % 2, c, i * P:(i + 1) * P],
                                                   ident[:])
                last.then_inc(turned_back, 1)

            def rank(g):
                tt = tiles_of(g)
                count = tt.stop - tt.start
                pe.wait_ge(mask_ready, g + 1)
                if g >= 1:
                    pe.wait_ge(slots_ready, g)
                nc.tensor.matmul(ps[:, 7, 0:count * E], before[:], mask[:, tt].rearrange("p i e -> p (i e)"),
                                 start=True, stop=False, skip_group_check=True)
                for i in range(count):
                    last = nc.tensor.matmul(rank_ps[:, i + 1:count + 1, :], ones[:],
                                            mask[:, tt.start + i:tt.start + i + 1, :].to_broadcast([P, count - i, E]),
                                            start=False, stop=(i == count - 1), skip_group_check=True)
                last.then_inc(ranks, 1)

            turn(0)
            style_rest()
            turn(1)
            logits_and_back(0)
            for n in range(2, PAIRS):
                if routed_at(n):
                    rank(routed_at(n) - 1)
                turn(n)
                logits_and_back(n - 1)
            rank(len(GROUPS) - 2)
            logits_and_back(PAIRS - 1)
            rank(len(GROUPS) - 1)

            def step(s, u, sure):
                if exists(s, 0) and sure:
                    i, k = u % 2, u % UNROLL
                    pe.wait_ge(got_in[k], 16 * (s // UNROLL + 1) if isinstance(s, int)
                               else ((s - k) * (16 // UNROLL) + 16))
                    if later(s, 2):
                        pe.wait_ge(hin_low, s - 1)
                    for c in range(DC):
                        for r in range(ETB):
                            last = nc.tensor.transpose(hin_ps[i][:, c * ET + r * P:c * ET + (r + 1) * P],
                                                       got[:, k, r, c * P:(c + 1) * P], ident[:])
                    last.then_inc(hin_t, 1)
                if exists(s, 1):
                    t, i = s - 1, (u - 1) % 2
                    def first_layer(side, need):
                        pe.wait_ge(w_ready, need)
                        pe.wait_ge(hin_low, t + 1)
                        for k in range(FC):
                            if later(s, 2) and k % 2 == 0:
                                pe.wait_ge(hid_read, (t - 1) * HB + (k // 2 + 1))
                            for c in range(DC):
                                tokens = slice(c * ET, (c + 1) * ET)
                                for w, against in ((0, (hin_hi, hin_lo)), (1, (hin_hi,))):
                                    off = side * 2 * WE + w * WE + c * FF + k * P
                                    for part in against:
                                        last = nc.tensor.matmul(hid_ps[:, k // 2, (k % 2) * ET:(k % 2 + 1) * ET],
                                                                wts[:, off:off + P], part[:, i, tokens],
                                                                start=(c == 0 and w == 0 and part is hin_hi),
                                                                stop=(c == DC - 1 and w == 1))
                            if k % 2 == 1:
                                last.then_inc(l1_done, 1)

                    if isinstance(t, int) and t == 0:
                        first_layer(0, 1)
                        pe.wait_ge(table_ready, 1)
                    else:
                        with if_real(pe, t, sure):
                            slot = pe.value_load(table[0:1, T_SLOT, bass.ds(t, 1)], min_val=0, max_val=1)
                            need = pe.value_load(table[0:1, T_NEED, bass.ds(t, 1)], min_val=1, max_val=E)
                            with pe.If(slot < 1):
                                first_layer(0, need)
                            with pe.Else():
                                first_layer(1, need)
                if exists(s, 2):
                    with if_real(pe, s - 2, sure):
                        t, i = s - 2, (u - 2) % 2
                        slot = pe.value_load(table[0:1, T_SLOT, bass.ds(t, 1)], min_val=0, max_val=1)
                        pe.wait_ge(hid_low, (t + 1) * 2)
                        if later(s, 4):
                            pe.wait_ge(y_biased, t - 1)
                        for r in range(ETB):
                            for k in range(FC):
                                tokens = slice(k * ET + r * P, k * ET + (r + 1) * P)
                                for part, against in ((hid_hi, (0, 1)), (hid_lo, (0,))):
                                    for w in against:
                                        off = slot * (2 * WE) + (w * WE + DC * FF + k * D)
                                        last = nc.tensor.matmul(y_ps[i][:, r * D:(r + 1) * D], part[:, i, tokens],
                                                                wts[:, bass.ds(off, D)],
                                                                start=(k == 0 and part is hid_hi and w == 0),
                                                                stop=(k == FC - 1 and part is hid_lo))
                        last.then_inc(l2_done, 1)

            tile_loop(pe, step)


_INS = ['x', 'condB_theta', 'condB_phi', 'itok_B_6_14', 'L1_cond_ln_g', 'L1_cond_ln_b', 'L1_cond_subj_emb',
        'L1_cond_hyp_w1', 'L1_cond_hyp_b1', 'L1_cond_hyp_w2', 'L1_cond_hyp_b2', 'L1_cond_sty_w1', 'L1_cond_sty_b1',
        'L1_cond_sty_w2', 'L1_cond_sty_b2', 'L1_cond_router_w', 'L1_cond_exp_w1', 'L1_cond_exp_b1',
        'L1_cond_exp_w2', 'L1_cond_exp_b2']


def kernel(**inputs):
    import numpy as _np
    import concourse.bacc as _bacc
    from concourse import mybir as _mybir
    from concourse.bass_utils import run_bass_kernel_spmd as _run

    nc = _bacc.Bacc("TRN2", target_bir_lowering=False, num_devices=1)
    arrays, args = {}, []
    for name in _INS:
        a = _np.ascontiguousarray(inputs[name])
        arrays[f"in_{name}_dram"] = a
        args.append(nc.dram_tensor(f"in_{name}_dram", a.shape, _mybir.dt.from_np(a.dtype), kind="ExternalInput").ap())
    args.append(nc.dram_tensor("out_0_dram", (N + 2 * P, D), F32, kind="ExternalOutput").ap())
    moe_kernel(nc, *args)
    r = _run(nc, [arrays], core_ids=[0])
    return r.results[0]["out_0_dram"][0:N].reshape(B, S, D)
```
